# Optimizing a Trainium2 kernel written in Bass

```python
import numpy as np
import jax
import jax.numpy as jnp

def _softmax(x, axis=-1):
    return jax.nn.softmax(x, axis=axis)

def _gelu(x):
    return jax.nn.gelu(x, approximate=True)

def _silu(x):
    return jax.nn.silu(x)

def _sigmoid(x):
    return jax.nn.sigmoid(x)

def _layernorm(x, axis=-1, eps=1e-05):
    m = jnp.mean(x, axis=axis, keepdims=True)
    v = jnp.var(x, axis=axis, keepdims=True)
    return (x - m) / jnp.sqrt(v + eps)

def _scatter_add(tgt, idx, src, axis=0):
    return tgt.at[idx].add(src)

def _segment_sum(src, seg, n):
    return jax.ops.segment_sum(src, seg, n)
kernel_name = 'mk_audio_tower_d1_tok_audfeat512_r4_8c3b47'

def setup_inputs(seed: int=0):
    np.random.seed(seed)
    _w = jnp.asarray

    def _rec_inputs():
        import jax
        import jax.numpy as jnp
        _rk = jax.random.key(seed)
        x = 7.22013e-05 + 1.00017 * jax.random.normal(jax.random.fold_in(_rk, 1), (16, 64, 250), jnp.float32)
        return x
    x = _rec_inputs()

    def _L0_tok_setup():
        import jax, jax.numpy as jnp
        import numpy as np
        B, C, T, D, K = (32, 64, 1024, 128, 3)
        key = jax.random.key(seed)
        ks = jax.random.split(key, 6)
        return {'x': jax.random.normal(ks[0], (B, C, T), dtype=jnp.float32), 'conv_w': jax.random.normal(ks[1], (C, 1, K), dtype=jnp.float32) * 0.1, 'conv_b': jax.random.normal(ks[2], (C,), dtype=jnp.float32) * 0.1, 'lin_w': jax.random.normal(ks[3], (D, C), dtype=jnp.float32) * (1.0 / np.sqrt(C)), 'lin_b': jax.random.normal(ks[4], (D,), dtype=jnp.float32) * 0.1, 'emb': jax.random.normal(ks[5], (C, D), dtype=jnp.float32), 'ln_g': jnp.ones((D,), dtype=jnp.float32), 'ln_b': jnp.zeros((D,), dtype=jnp.float32)}
    _L0_tok_all = _L0_tok_setup()
    _L0_tok_in = {k: v for k, v in _L0_tok_all.items() if k in ('conv_w', 'conv_b', 'lin_w', 'lin_b', 'emb', 'ln_g', 'ln_b')}
    del _L0_tok_all

    def _L0_attn_setup():
        import jax, jax.numpy as jnp
        import numpy as np
        SCALE = 64 ** 0.5
        key = jax.random.key(seed)
        kx, kw = jax.random.split(key)
        B, S, D, O = (8, 512, 128, 128)
        x = jax.random.normal(kx, (B, S, D), dtype=jnp.float32)
        kernel = jax.random.normal(kw, (3, D, O), dtype=jnp.float32) * 0.02
        return {'x': x, 'kernel': kernel}
    _L0_attn_all = _L0_attn_setup()
    _L0_attn_in = {k: v for k, v in _L0_attn_all.items() if k in ('kernel',)}
    del _L0_attn_all

    def _L0_ffn_setup():
        import jax, jax.numpy as jnp
        import numpy as np
        T = 128
        B = 64
        C = 256

        def _triu_apply(x, W, b):
            Wm = jnp.tril(W)
            return jnp.einsum('bct,st->bcs', x, Wm) + b
        key = jax.random.key(seed)
        ks = jax.random.split(key, 5)
        x = jax.random.normal(ks[0], (B, C, T), dtype=jnp.float32)
        scale = 1.0 / jnp.sqrt(jnp.arange(1, T + 1, dtype=jnp.float32))[:, None]
        W1 = jax.random.uniform(ks[1], (T, T), jnp.float32, -1.0, 1.0) * scale
        b1 = jax.random.uniform(ks[2], (T,), jnp.float32, -1.0, 1.0) * scale[:, 0]
        W2 = jax.random.uniform(ks[3], (T, T), jnp.float32, -1.0, 1.0) * scale
        b2 = jax.random.uniform(ks[4], (T,), jnp.float32, -1.0, 1.0) * scale[:, 0]
        return {'x': x, 'W1': W1, 'b1': b1, 'W2': W2, 'b2': b2}
    _L0_ffn_all = _L0_ffn_setup()
    _L0_ffn_in = {k: v for k, v in _L0_ffn_all.items() if k in ('W1', 'b1', 'W2', 'b2')}
    del _L0_ffn_all
    return {'x': x, 'L0_tok_conv_w': _L0_tok_in['conv_w'], 'L0_tok_conv_b': _L0_tok_in['conv_b'], 'L0_tok_lin_w': _L0_tok_in['lin_w'], 'L0_tok_lin_b': _L0_tok_in['lin_b'], 'L0_tok_emb': _L0_tok_in['emb'], 'L0_tok_ln_g': _L0_tok_in['ln_g'], 'L0_tok_ln_b': _L0_tok_in['ln_b'], 'L0_attn_kernel': _L0_attn_in['kernel'], 'L0_ffn_W1': _L0_ffn_in['W1'], 'L0_ffn_b1': _L0_ffn_in['b1'], 'L0_ffn_W2': _L0_ffn_in['W2'], 'L0_ffn_b2': _L0_ffn_in['b2']}

def reference(x, L0_tok_conv_w, L0_tok_conv_b, L0_tok_lin_w, L0_tok_lin_b, L0_tok_emb, L0_tok_ln_g, L0_tok_ln_b, L0_attn_kernel, L0_ffn_W1, L0_ffn_b1, L0_ffn_W2, L0_ffn_b2):
    import jax
    import jax.numpy as jnp

    def _L0_tok_ref(x, conv_w, conv_b, lin_w, lin_b, emb, ln_g, ln_b):
        import jax, jax.numpy as jnp
        import numpy as np
        B, C, T, D, K = (32, 64, 1024, 128, 3)
        pad = K // 2
        x_sp = jax.lax.conv_general_dilated(x, conv_w, window_strides=(1,), padding=[(pad, pad)], dimension_numbers=('NCH', 'OIH', 'NCH'), feature_group_count=C) + conv_b[None, :, None]
        x_t = jnp.swapaxes(x_sp, 1, 2)
        x_mixed = jnp.einsum('btc,dc->btd', x_t, lin_w) + lin_b
        x_mixed = x_mixed + emb.mean(axis=0)
        mu = x_mixed.mean(axis=-1, keepdims=True)
        var = x_mixed.var(axis=-1, keepdims=True)
        x_n = (x_mixed - mu) * jax.lax.rsqrt(var + 1e-05)
        return x_n * ln_g + ln_b

    def _L0_attn_ref(x, kernel):
        import jax, jax.numpy as jnp
        import numpy as np
        SCALE = 64 ** 0.5
        WQ = jnp.einsum('bsd,do->bso', x, kernel[0])
        WK = jnp.einsum('bsd,do->bso', x, kernel[1])
        WV = jnp.einsum('bsd,do->bso', x, kernel[2])
        QK = jnp.einsum('bso,bto->bst', WQ, WK)
        row_sums = jnp.sum(QK, axis=2)
        c0 = jnp.argmin(row_sums[0])
        A = jax.nn.softmax(QK / SCALE, axis=-1)
        row_mask = (jnp.arange(QK.shape[1]) == c0)[None, :, None]
        A = jnp.where(row_mask, jnp.zeros((), A.dtype), A)
        V = jnp.einsum('bst,bto->bso', A, WV)
        return V

    def _L0_ffn_ref(x, W1, b1, W2, b2):
        import jax, jax.numpy as jnp
        import numpy as np
        T = 128
        B = 64
        C = 256

        def _triu_apply(x, W, b):
            Wm = jnp.tril(W)
            return jnp.einsum('bct,st->bcs', x, Wm) + b
        h = _triu_apply(x, W1, b1)
        h = jax.nn.gelu(h, approximate=False)
        return _triu_apply(h, W2, b2)
    h = _L0_tok_ref(x, L0_tok_conv_w, L0_tok_conv_b, L0_tok_lin_w, L0_tok_lin_b, L0_tok_emb, L0_tok_ln_g, L0_tok_ln_b)
    h = h + _L0_attn_ref(_layernorm(h, axis=-1), L0_attn_kernel)
    h = h + _L0_ffn_ref(_layernorm(h, axis=-1), L0_ffn_W1, L0_ffn_b1, L0_ffn_W2, L0_ffn_b2)
    return h

_drawn_inputs = setup_inputs


def setup_inputs(seed=0):
    import zlib

    import numpy as np

    out = dict(_drawn_inputs(seed))
    spreads = {'L0_tok_ln_g': (1.0, 0.2), 'L0_tok_ln_b': (0.0, 0.1)}
    factors = {}
    for name, (base, spread) in spreads.items():
        noise = np.random.default_rng([zlib.crc32(name.encode()), seed]).standard_normal(out[name].shape)
        drawn = base * np.exp(spread * noise) if base else spread * noise
        out[name] = jnp.asarray(drawn.astype(out[name].dtype))
    for name, factor in factors.items():
        out[name] = (out[name] * factor).astype(out[name].dtype)
    return out
```

```python
from contextlib import ExitStack

import concourse.bass as bass
from concourse import mybir

ALU = mybir.AluOpType
ACT = mybir.ActivationFunctionType
AX_X = mybir.AxisListType.X
F32 = mybir.dt.float32
BF16 = mybir.dt.bfloat16

EPS = 1e-5
SCORE_SCALE = 1.0 / 64 ** 0.5


def audio_tower(nc, x, tok_pack, emb_pack, weights, rows, out):
    NB, C, T = x.shape
    D = out.shape[2]
    H = T // 2
    NP = NB // 2
    DV = D + 1
    BIG = float(4 * T)

    x_pairs = x.rearrange("(k h) c t -> k (h c) t", h=2)
    out_pairs = out.rearrange("(j b) (a p) d -> j p (b a) d", b=2, p=H)

    with ExitStack() as ctx:
        def sb(name, shape, dt=F32):
            return ctx.enter_context(nc.sbuf_tensor(name, shape, dt))

        def sem(name):
            return ctx.enter_context(nc.semaphore(name))

        def bank(name):
            return ctx.enter_context(nc.psum_tensor(name, [128, 512], F32))

        bank_x = [bank("bank_x0"), bank("bank_x1")]
        bank_np, bank_v, bank_s, bank_at, bank_o, bank_misc = (
            bank(n) for n in ("bank_np", "bank_v", "bank_s", "bank_at", "bank_o", "bank_misc"))
        x_ps = [t[0:H, 0:2 * D].rearrange("p (a d) -> p a d", a=2) for t in bank_x]
        n1t_ps = bank_np[:, 0:T]
        p_ps = bank_np[:, 0:T]
        v_ps = bank_v[0:H, 0:2 * D].rearrange("p (a d) -> p a d", a=2)
        s_ps = bank_s[0:H, 0:2 * T].rearrange("p (a t) -> p a t", a=2)
        at_ps = bank_at[0:H, 0:2 * T].rearrange("p (c s) -> p c s", c=2)
        o_ps = bank_o[0:H, 0:2 * (D + 2)].rearrange("p (a d) -> p a d", a=2)
        t2_ps = [t[:, 0:2 * T] for t in bank_x]
        f1_ps = [bank_misc[:, 0:2 * T], bank_v[:, 0:2 * T]]
        y_ps = [t[0:H, :].rearrange("p (n d) -> p n d", d=D) for t in (bank_np, bank_at)]

        tok_w = sb("tok_w", [128, D + 4])
        lin_t = tok_w[:, 0:D]
        conv_b = tok_w[:, D + 3:D + 4]
        lin_c = sb("lin_c", [128, D])
        lin_mean = sb("lin_mean", [128, 1])
        emb_b = sb("emb_b", [C + 1, D])
        mean_w = sb("mean_w", [C + 1, C + 1])
        cb = sb("cb", [C + 1, D])
        cb_sum = sb("cb_sum", [C + 1, 1])
        cb_mean = sb("cb_mean", [C + 1, 1])
        cb_rest = sb("cb_rest", [C + 1, D])
        cb_rest2 = sb("cb_rest2", [C + 1, D])
        cb_hi = sb("cb_hi", [C + 1, D], BF16)
        cb_mid = sb("cb_mid", [C + 1, D], BF16)
        cb_rows = sb("cb_rows", [C + 1, D], BF16)
        ones_b = sb("ones_b", [C + 1, H], BF16)
        w_sb = sb("w_sb", [128, 5 * D + 1])
        wq_t, wk_t, w_v, w1_t, w2_t = (w_sb[:, n * D:(n + 1) * D] for n in range(5))
        b1_col = w_sb[:, 5 * D:5 * D + 1]
        qk_w = sb("qk_w", [128, D])
        rows_sb = sb("rows_sb", [1, 3 * D])
        ones_row = sb("ones_row", [1, H])
        gamma = sb("gamma", [H, D])
        beta2 = sb("beta2", [H, 2, D])
        b2_2 = sb("b2_2", [H, 2, D])
        ident = sb("ident", [128, 128])
        neg_half = sb("neg_half", [H, 4])
        eps = sb("eps", [H, 4])
        token_row = sb("token_row", [1, T])
        token_col = sb("token_col", [H, 2])

        x_slot = sb("x_slot", [128, T + 2])
        tap0 = sb("tap0", [128, T])
        tap1 = sb("tap1", [128, T])
        tap2 = sb("tap2", [128, T])
        tap01 = sb("tap01", [128, T])
        xc = sb("xc", [128, T])
        squared = [sb(f"squared{p}", [H, 2, D]) for p in range(2)]
        ssq = [sb(f"ssq{p}", [H, 2]) for p in range(2)]
        var_x = [sb(f"var_x_{p}", [H, 2]) for p in range(2)]
        rstd_x = [sb(f"rstd_x{p}", [H, 2]) for p in range(2)]
        scaled = [sb(f"scaled{p}", [H, 2, D]) for p in range(2)]
        h_all = sb("h_all", [H, NB, 2 * D])
        hb_all = sb("hb_all", [H, NB, 2 * D])
        hb_pairs = hb_all[:, :, :].rearrange("p (j b) d -> p j (b d)", b=2)
        bn1 = [sb(f"bn1_{p}", [H, 2, 6]) for p in range(2)]
        mv1 = [sb(f"mv1_{p}", [H, 2, 2]) for p in range(2)]
        var1 = [sb(f"var1_{p}", [H, 2]) for p in range(2)]
        rstd1 = [sb(f"rstd1_{p}", [H, 2]) for p in range(2)]
        n1 = [sb(f"n1_{p}", [H, 2, D]) for p in range(2)]
        n1t = [sb(f"n1t{p}", [128, T]) for p in range(2)]
        pt = [sb(f"pt{p}", [128, T]) for p in range(2)]
        v_sb = [sb(f"v{p}", [H, 2, DV]) for p in range(2)]
        neg_max = [sb(f"neg_max{p}", [H, 2]) for p in range(2)]
        a_sb = [sb(f"a{p}", [H, 2, T]) for p in range(2)]
        at_sb = [sb(f"at{p}", [H, 2, T]) for p in range(2)]
        row_sum = sb("row_sum", [H, 2])
        sum_row = sb("sum_row", [1, T])
        least = sb("least", [1, 1])
        cand0 = sb("cand0", [1, T])
        cand = sb("cand", [1, T])
        c0 = sb("c0", [1, 1])
        c0_col = sb("c0_col", [H, 1])
        keep = sb("keep", [H, 2])
        rinv = sb("rinv", [H, 2])
        rinv_keep = sb("rinv_keep", [H, 2])
        bn2 = [sb(f"bn2_{p}", [H, 4, 6]) for p in range(2)]
        mv2 = [sb(f"mv2_{p}", [H, 4, 2]) for p in range(2)]
        var2 = [sb(f"var2_{p}", [H, 4]) for p in range(2)]
        rstd2 = [sb(f"rstd2_{p}", [H, 4]) for p in range(2)]
        n2 = [sb(f"n2_{p}", [H, 4, D]) for p in range(2)]
        n2t = [sb(f"n2t{p}", [128, 2 * T]) for p in range(2)]
        g_sb = [sb(f"g{p}", [128, 2 * T]) for p in range(2)]

        landed_x, landed_tok, landed_emb, landed_w, landed_rows = (
            sem("landed_" + n) for n in ("x", "tok", "emb", "w", "rows"))
        out_done = sem("out_done")
        consts_ready, dve_consts = sem("consts_ready"), sem("dve_consts")
        lin_centred, cb_mm, cb_ready = sem("lin_centred"), sem("cb_mm"), sem("cb_ready")
        qk_mm, qk_ready, rows_mm, rows_ready = sem("qk_mm"), sem("qk_ready"), sem("rows_mm"), sem("rows_ready")
        tri_ready, mean_w_ready = sem("tri_ready"), sem("mean_w_ready")
        dve_step, pool_step = sem("dve_step"), sem("pool_step")
        slot_read, conv_ready = sem("slot_read"), sem("conv_ready")
        x_mm, x_squared, rstd_x_ready, x_scaled, h_ready = (
            sem(n) for n in ("x_mm", "x_squared", "rstd_x_ready", "x_scaled", "h_ready"))
        stats1, rstd1_ready, n1_ready, n1t_mm, n1t_ready = (
            sem(n) for n in ("stats1", "rstd1_ready", "n1_ready", "n1t_mm", "n1t_ready"))
        p_mm, p_ready, v_mm, v_ready, s_mm, max_ready, exp_ready = (
            sem(n) for n in ("p_mm", "p_ready", "v_mm", "v_ready", "s_mm", "max_ready", "exp_ready"))
        at_mm, at_ready, o_mm, resid_ready, hb_ready = (
            sem(n) for n in ("at_mm", "at_ready", "o_mm", "resid_ready", "hb_ready"))
        sums_read, sums_t, c0_ready, c0_bcast, keep_ready = (
            sem(n) for n in ("sums_read", "sums_t", "c0_ready", "c0_bcast", "keep_ready"))
        stats2, rstd2_ready, n2_ready, t2_mm, n2t_ready, f1_mm, gelu_ready, y_mm, y_ready = (
            sem(n) for n in ("stats2", "rstd2_ready", "n2_ready", "t2_mm", "n2t_ready", "f1_mm",
                             "gelu_ready", "y_mm", "y_ready"))
        N_CONSTS = 11

        block = ctx.enter_context(nc.Block())

        @block.sync
        def _(sp):
            sp.dma_start(x_slot[:, 1:T + 1], x_pairs[0]).then_inc(landed_x, 16)
            sp.dma_start(w_sb[:, :], weights).then_inc(landed_w, 16)
            with sp.Fori(1, NP) as k:
                sp.wait_ge(slot_read, k)
                sp.dma_start(x_slot[:, 1:T + 1], x_pairs[k]).then_inc(landed_x, 16)
            with sp.Fori(0, NP) as j:
                sp.wait_ge(y_ready, j + 1)
                sp.dma_start(out_pairs[j], hb_pairs[:, j, :].rearrange("p (n d) -> p n d", d=D))\
                    .then_inc(out_done, 16)
            sp.wait_ge(out_done, 16 * NP)

        @block.gpsimd
        def _(pool):
            pool.memset(x_slot[:, 0:1], 0.0).then_inc(consts_ready, 1)
            pool.memset(x_slot[:, T + 1:T + 2], 0.0).then_inc(consts_ready, 1)
            pool.memset(neg_half[:, :], -0.5).then_inc(consts_ready, 1)
            pool.memset(eps[:, :], EPS).then_inc(consts_ready, 1)
            pool.wait_ge(consts_ready, 4)

            def conv_taps(k):
                for n, t in enumerate((tap0, tap1, tap2)):
                    w = tok_w[:, D + n:D + n + 1]
                    ins = pool.tensor_scalar(t[:, :], x_slot[:, n:n + T], w, conv_b if n == 0 else 0.0,
                                             ALU.mult, ALU.add)
                    ins.then_inc(slot_read if n == 2 else pool_step, 1)

            def conv_sum(k, nsteps):
                pool.wait_ge(pool_step, nsteps)
                pool.wait_ge(slot_read, k + 1)
                pool.tensor_tensor(tap01[:, :], tap0[:, :], tap1[:, :], ALU.add).then_inc(pool_step, 1)
                pool.wait_ge(pool_step, nsteps + 1)
                if not isinstance(k, int) or k > 0:
                    pool.wait_ge(x_mm, 2 * k)
                pool.tensor_tensor(xc[:, :], tap01[:, :], tap2[:, :], ALU.add).then_inc(conv_ready, 1)

            def root_x(b, par, n):
                pool.wait_ge(x_squared, 2 * b + 2)
                pool.tensor_tensor(var_x[par][:, :], ssq[par][:, :], eps[:, 0:2], ALU.add).then_inc(pool_step, 1)
                pool.wait_ge(pool_step, n + 1)
                pool.tensor_tensor(rstd_x[par][:, :], var_x[par][:, :], neg_half[:, 0:2], ALU.pow).then_inc(rstd_x_ready, 1)

            def root1(b, par, n):
                pool.wait_ge(stats1, b + 1)
                pool.tensor_tensor(var1[par][:, :], mv1[par][:, :, 1], eps[:, 0:2], ALU.add).then_inc(pool_step, 1)
                pool.wait_ge(pool_step, n + 1)
                pool.tensor_tensor(rstd1[par][:, :], var1[par][:, :], neg_half[:, 0:2], ALU.pow).then_inc(rstd1_ready, 1)

            def add_beta(b, par):
                pool.wait_ge(x_scaled, b + 1)
                pool.tensor_tensor(h_all[:, b, :], scaled[par][:, :, :].rearrange("p a d -> p (a d)"),
                                   beta2[:, :, :].rearrange("p a d -> p (a d)"), ALU.add).then_inc(h_ready, 1)

            def add_b2(b):
                pool.wait_ge(resid_ready, b + 1)
                pool.tensor_tensor(hb_all[:, b, :], h_all[:, b, :],
                                   b2_2[:, :, :].rearrange("p a d -> p (a d)"), ALU.add).then_inc(hb_ready, 1)

            pool.wait_ge(landed_tok, 16)
            pool.wait_ge(landed_x, 16)
            conv_taps(0)
            conv_sum(0, 2)
            pool.memset(ones_b[:, :], 1.0).then_inc(consts_ready, 1)
            pool.memset(ones_row[:, :], 1.0).then_inc(consts_ready, 1)
            pool.memset(ident[:, :], 0.0).then_inc(consts_ready, 1)
            pool.wait_ge(consts_ready, 7)
            pool.affine_select(out=ident[:, :], in_=ident[:, :], compare_op=ALU.not_equal, fill=1.0,
                               base=0, pattern=[[-1, 128]], channel_multiplier=1).then_inc(consts_ready, 1)
            for p in range(2):
                pool.memset(v_sb[p][:, :, D:DV], 1.0).then_inc(consts_ready, 1)
            pool.wait_ge(landed_x, 32)
            conv_taps(1)
            pool.iota(token_row[:, :], pattern=[[1, T]], base=0, channel_multiplier=0,
                      allow_small_or_imprecise_dtypes=True).then_inc(consts_ready, 1)
            pool.iota(token_col[:, :], pattern=[[H, 2]], base=0, channel_multiplier=1,
                      allow_small_or_imprecise_dtypes=True).then_inc(dve_consts, 1)
            pool.wait_ge(landed_w, 16)
            for w in (w1_t, w2_t):
                pool.affine_select(out=w, in_=w, compare_op=ALU.is_ge, fill=0.0, base=0,
                                   pattern=[[1, D]], channel_multiplier=-1).then_inc(tri_ready, 1)

            n = 3
            root_x(0, 0, n + 2); n += 1
            pool.wait_ge(rows_ready, 3)
            add_beta(0, 0)
            root_x(1, 1, n + 2); n += 1
            root1(0, 0, n + 2); n += 1
            add_beta(1, 1)
            n += 2
            conv_sum(1, n); n += 1
            root1(1, 1, n); n += 1
            pool.wait_ge(landed_x, 48)
            conv_taps(2); n += 2
            root_x(2, 0, n); n += 1
            add_beta(2, 0)
            conv_sum(2, n); n += 1
            root1(2, 0, n); n += 1
            root_x(3, 1, n); n += 1
            add_beta(3, 1)
            n_loop = n
            PER_PAIR = 2 + 1 + 4

            def even_step(b, k, n, conv):
                root1(b + 1, 1, n)
                root_x(b + 2, 0, n + 1)
                add_beta(b + 2, 0)
                if conv:
                    pool.wait_ge(landed_x, 16 * (k + 3))
                add_b2(b - 2)
                if conv:
                    conv_taps(k + 2)
                    n = n + 2
                return n + 2

            def odd_step(b, k, n, conv):
                root1(b + 1, 0, n)
                if conv:
                    conv_sum(k + 2, n + 1)
                    n = n + 1
                root_x(b + 2, 1, n + 1)
                add_beta(b + 2, 1)
                add_b2(b - 2)
                return n + 2

            with pool.Fori(1, NP - 2) as k:
                at = (k - 1) * PER_PAIR + n_loop
                at = even_step(2 * k, k, at, True)
                odd_step(2 * k + 1, k, at, True)
            n = n_loop + (NP - 3) * PER_PAIR
            n = even_step(NB - 4, NP - 2, n, False)
            n = odd_step(NB - 3, NP - 2, n, False)
            root1(NB - 1, 1, n)
            n += 1
            for b in range(NB - 4, NB - 1):
                add_b2(b)

            def root2(j, par, n):
                pool.wait_ge(stats2, j + 1)
                pool.tensor_tensor(var2[par][:, :], mv2[par][:, :, 1], eps[:, :], ALU.add).then_inc(pool_step, 1)
                pool.wait_ge(pool_step, n + 1)
                pool.tensor_tensor(rstd2[par][:, :], var2[par][:, :], neg_half[:, :], ALU.pow).then_inc(rstd2_ready, 1)

            root2(0, 0, n)
            root2(1, 1, n + 1)
            add_b2(NB - 1)
            with pool.Fori(1, NP // 2) as m:
                for par in range(2):
                    root2(2 * m + par, par, 2 * m + par + n)

        @block.tensor
        def _(pe):
            def project(b, par):
                if not isinstance(b, int) or b >= 2:
                    pe.wait_ge(x_scaled, b - 1)
                half = slice(par * C, (par + 1) * C)
                for a in range(2):
                    nc.tensor.matmul(x_ps[par][:, a, :], xc[half, a * H:(a + 1) * H], lin_c[half, :],
                                     start=True, stop=False)
                    last = nc.tensor.matmul(x_ps[par][:, a, :], ones_b[:, :], cb_rows[:, :],
                                            start=False, stop=True)
                last.then_inc(x_mm, 1)

            def turn_n1(b, par):
                pe.wait_ge(n1_ready, b + 1)
                if not isinstance(b, int) or b >= 1:
                    pe.wait_ge(p_ready, b)
                for a in range(2):
                    last = nc.tensor.transpose(n1t_ps[:, a * H:(a + 1) * H], n1[par][:, a, :], ident[0:H, 0:H])
                last.then_inc(n1t_mm, 1)

            def queries(b, par):
                pe.wait_ge(n1t_ready, b + 1)
                nc.tensor.matmul(p_ps, qk_w[:, :], n1t[par][:, :], start=True, stop=True).then_inc(p_mm, 1)

            def values(b, par):
                if not isinstance(b, int) or b >= 1:
                    pe.wait_ge(v_ready, b)
                for a in range(2):
                    last = nc.tensor.matmul(v_ps[:, a, :], n1t[par][:, a * H:(a + 1) * H], w_v,
                                            start=True, stop=True)
                last.then_inc(v_mm, 1)

            def scores(b, par):
                pe.wait_ge(p_ready, b + 1)
                if not isinstance(b, int) or b >= 1:
                    pe.wait_ge(exp_ready, b)
                if isinstance(b, int) and b == 1:
                    pe.wait_ge(sums_read, 1)
                for a in range(2):
                    last = nc.tensor.matmul(s_ps[:, a, :], pt[par][:, a * H:(a + 1) * H], n1t[par][:, :],
                                            start=True, stop=True)
                last.then_inc(s_mm, 1)

            def turn_a(b, par):
                pe.wait_ge(exp_ready, b + 1)
                if not isinstance(b, int) or b >= 1:
                    pe.wait_ge(at_ready, b)
                for a in range(2):
                    for c in range(2):
                        last = nc.tensor.transpose(at_ps[:, c, a * H:(a + 1) * H],
                                                   a_sb[par][:, a, c * H:(c + 1) * H], ident[0:H, 0:H])
                last.then_inc(at_mm, 1)

            def attend(b, par):
                pe.wait_ge(at_ready, b + 1)
                pe.wait_ge(v_ready, b + 1)
                if not isinstance(b, int) or b >= 1:
                    pe.wait_ge(resid_ready, b)
                for a in range(2):
                    for c in range(2):
                        last = nc.tensor.matmul(o_ps[:, a, 0:DV], at_sb[par][:, c, a * H:(a + 1) * H],
                                                v_sb[par][:, c, :], start=(c == 0), stop=(c == 1))
                last.then_inc(o_mm, 1)

            def step(i, par, first=False, pair=None):
                turn_n1(i, par)
                if pair is not None:
                    pe.wait_ge(conv_ready, pair + 1)
                    project(i + 2, par)
                queries(i, par)
                values(i, par)
                if not first:
                    turn_a(i - 1, 1 - par)
                scores(i, par)
                if not first:
                    attend(i - 1, 1 - par)

            pe.wait_ge(consts_ready, 8)
            pe.wait_ge(mean_w_ready, 2)
            pe.wait_ge(landed_emb, 16)
            nc.tensor.matmul(bank_misc[0:C + 1, 0:D], mean_w[:, :], emb_b[:, :], start=True, stop=True)\
                .then_inc(cb_mm, 1)
            pe.wait_ge(cb_ready, 3)
            pe.wait_ge(lin_centred, 1)
            pe.wait_ge(conv_ready, 1)
            project(0, 0)
            project(1, 1)
            pe.wait_ge(landed_rows, 16)
            nc.tensor.matmul(bank_misc[0:H, 0:3 * D], ones_row[:, :], rows_sb[:, :], start=True, stop=True)\
                .then_inc(rows_mm, 1)
            pe.wait_ge(landed_w, 16)
            nc.tensor.matmul(bank_v[:, 0:D], wq_t, wk_t, start=True, stop=True).then_inc(qk_mm, 1)
            pe.wait_ge(qk_ready, 1)
            pe.wait_ge(consts_ready, 10)

            step(0, 0, first=True, pair=1)
            step(1, 1, pair=1)
            pe.wait_ge(sums_read, 1)
            for a in range(2):
                last = nc.tensor.transpose(bank_misc[0:1, a * H:(a + 1) * H], row_sum[:, a:a + 1], ident[0:H, 0:H])
            last.then_inc(sums_t, 1)
            pe.wait_ge(c0_ready, 1)
            nc.tensor.matmul(bank_misc[0:H, 0:1], ones_row[:, :], c0[:, :], start=True, stop=True).then_inc(c0_bcast, 1)

            with pe.Fori(1, NP - 1) as k:
                step(2 * k, 0, pair=k + 1)
                step(2 * k + 1, 1, pair=k + 1)
            step(NB - 2, 0)
            step(NB - 1, 1)
            turn_a(NB - 1, 1)
            attend(NB - 1, 1)

            def turn_n2(j, par):
                pe.wait_ge(n2_ready, j + 1)
                if not isinstance(j, int) or j >= 2:
                    pe.wait_ge(n2t_ready, j - 1)
                for n in range(4):
                    last = nc.tensor.transpose(t2_ps[par][:, n * H:(n + 1) * H], n2[par][:, n, :], ident[0:H, 0:H])
                last.then_inc(t2_mm, 1)

            def up(j, par):
                pe.wait_ge(n2t_ready, j + 1)
                if not isinstance(j, int) or j >= 2:
                    pe.wait_ge(gelu_ready, j - 1)
                nc.tensor.matmul(f1_ps[par], w1_t, n2t[par][:, :], start=True, stop=True).then_inc(f1_mm, 1)

            def down(j, par):
                pe.wait_ge(gelu_ready, j + 1)
                if isinstance(j, int) and j >= 2:
                    pe.wait_ge(y_ready, j - 1)
                for n in range(4):
                    last = nc.tensor.matmul(y_ps[par][:, n, :], g_sb[par][:, n * H:(n + 1) * H], w2_t,
                                            start=True, stop=True)
                last.then_inc(y_mm, 1)

            pe.wait_ge(tri_ready, 2)
            turn_n2(0, 0)
            turn_n2(1, 1)
            up(0, 0)
            turn_n2(2, 0)
            up(1, 1)
            down(0, 0)
            with pe.Fori(1, NP // 2 - 1) as m:
                for par in range(2):
                    turn_n2(2 * m + par + 1, 1 - par)
                    up(2 * m + par, par)
                    down(2 * m + par - 1, 1 - par)
            turn_n2(NP - 1, 1)
            up(NP - 2, 0)
            down(NP - 3, 1)
            up(NP - 1, 1)
            down(NP - 2, 0)
            down(NP - 1, 1)

        @block.scalar
        def _(act):
            act.dma_start(tok_w[:, :], tok_pack).then_inc(landed_tok, 16)
            act.dma_start(emb_b[:, :], emb_pack).then_inc(landed_emb, 16)
            act.dma_start(rows_sb[:, :], rows).then_inc(landed_rows, 16)

            def squares(b, par):
                act.wait_ge(x_mm, b + 1)
                for a in range(2):
                    nc.scalar.activation(squared[par][:, a, :], x_ps[par][:, a, :], ACT.Square, scale=float(D) ** -0.5,
                                         accum_out=ssq[par][:, a:a + 1]).then_inc(x_squared, 1)

            def out_n1t(b, par):
                act.wait_ge(n1t_mm, b + 1)
                if not isinstance(b, int) or b >= 2:
                    act.wait_ge(s_mm, b - 1)
                nc.scalar.activation(n1t[par][:, :], n1t_ps, ACT.Copy).then_inc(n1t_ready, 1)

            def out_p(b, par):
                act.wait_ge(p_mm, b + 1)
                nc.scalar.activation(pt[par][:, :], p_ps, ACT.Copy).then_inc(p_ready, 1)

            def out_v(b, par):
                act.wait_ge(v_mm, b + 1)
                if not isinstance(b, int) or b >= 2:
                    act.wait_ge(o_mm, b - 1)
                nc.scalar.activation(v_sb[par][:, :, 0:D], v_ps, ACT.Copy).then_inc(v_ready, 1)

            def exps(b, par):
                act.wait_ge(max_ready, b + 1)
                if isinstance(b, int) and b == 0:
                    act.wait_ge(sums_read, 1)
                for a in range(2):
                    last = nc.scalar.activation(a_sb[par][:, a, :], s_ps[:, a, :], ACT.Exp,
                                                bias=neg_max[par][:, a:a + 1])
                last.then_inc(exp_ready, 1)

            def out_at(b, par):
                act.wait_ge(at_mm, b + 1)
                nc.scalar.activation(at_sb[par][:, :, :], at_ps, ACT.Copy).then_inc(at_ready, 1)

            def step(i, par, first=False, more=True):
                out_n1t(i, par)
                if not first:
                    exps(i - 1, 1 - par)
                out_p(i, par)
                if more:
                    squares(i + 2, par)
                out_v(i, par)
                if not first:
                    out_at(i - 1, 1 - par)

            squares(0, 0)
            squares(1, 1)
            act.wait_ge(qk_mm, 1)
            nc.scalar.activation(qk_w[:, :], bank_v[:, 0:D], ACT.Copy, scale=SCORE_SCALE).then_inc(qk_ready, 1)
            step(0, 0, first=True)
            step(1, 1)
            with act.Fori(1, NP - 1) as k:
                step(2 * k, 0)
                step(2 * k + 1, 1)
            step(NB - 2, 0, more=False)
            step(NB - 1, 1, more=False)
            exps(NB - 1, 1)
            out_at(NB - 1, 1)

            def out_n2t(j, par):
                act.wait_ge(t2_mm, j + 1)
                if not isinstance(j, int) or j >= 2:
                    act.wait_ge(f1_mm, j - 1)
                nc.scalar.activation(n2t[par][:, :], t2_ps[par], ACT.Copy).then_inc(n2t_ready, 1)

            def gelu(j, par):
                act.wait_ge(f1_mm, j + 1)
                nc.scalar.activation(g_sb[par][:, :], f1_ps[par], ACT.Gelu, bias=b1_col).then_inc(gelu_ready, 1)

            out_n2t(0, 0)
            out_n2t(1, 1)
            gelu(0, 0)
            with act.Fori(0, NP // 2 - 1) as m:
                for par in (1, 0):
                    j = 2 * m + (2 - par)
                    out_n2t(j + 1, 1 - par)
                    gelu(j, par)
            gelu(NP - 1, 1)

        @block.vector
        def _(dve):
            count = {"n": 0}

            def chain(ins):
                count["n"] += 1
                ins.then_inc(dve_step, 1)
                dve.wait_ge(dve_step, count["n"])

            nc.vector.memset(mean_w[0:C, :], 1.0 / C).then_inc(mean_w_ready, 1)
            nc.vector.memset(mean_w[C:C + 1, :], 1.0).then_inc(mean_w_ready, 1)
            chain(nc.vector.memset(cb_rows[:, :], 0.0))
            dve.wait_ge(landed_tok, 16)
            chain(nc.vector.tensor_reduce(lin_mean[:, :], lin_t, AX_X, ALU.add))
            chain(nc.vector.tensor_scalar(lin_mean[:, :], lin_mean[:, :], 1.0 / D, None, ALU.mult))
            nc.vector.tensor_scalar(lin_c[:, :], lin_t, lin_mean[:, :], None, ALU.subtract).then_inc(lin_centred, 1)
            dve.wait_ge(cb_mm, 1)
            chain(nc.vector.tensor_reduce(cb_sum[:, :], bank_misc[0:C + 1, 0:D], AX_X, ALU.add))
            chain(nc.vector.tensor_scalar(cb_mean[:, :], cb_sum[:, :], 1.0 / D, None, ALU.mult))
            chain(nc.vector.tensor_scalar(cb[:, :], bank_misc[0:C + 1, 0:D], cb_mean[:, :], None, ALU.subtract))
            chain(nc.vector.tensor_copy(cb_hi[:, :], cb[:, :]))
            chain(nc.vector.tensor_tensor(cb_rest[:, :], cb[:, :], cb_hi[:, :], ALU.subtract))
            chain(nc.vector.tensor_copy(cb_mid[:, :], cb_rest[:, :]))
            chain(nc.vector.tensor_tensor(cb_rest2[:, :], cb_rest[:, :], cb_mid[:, :], ALU.subtract))
            nc.vector.tensor_copy(cb_rows[0:1, :], cb_hi[0:1, :]).then_inc(cb_ready, 1)
            nc.vector.tensor_copy(cb_rows[32:33, :], cb_mid[32:33, :]).then_inc(cb_ready, 1)
            nc.vector.tensor_copy(cb_rows[64:65, :], cb_rest2[64:65, :]).then_inc(cb_ready, 1)

            def scale_x(b, par):
                dve.wait_ge(rstd_x_ready, b + 1)
                if not isinstance(b, int) or b >= 2:
                    dve.wait_ge(h_ready, b - 1)
                for a in range(2):
                    last = nc.vector.scalar_tensor_tensor(scaled[par][:, a, :], x_ps[par][:, a, :],
                                                          rstd_x[par][:, a:a + 1], gamma[:, :],
                                                          ALU.mult, ALU.mult)
                last.then_inc(x_scaled, 1)

            def stats_1(b, par):
                dve.wait_ge(h_ready, b + 1)
                for a in range(2):
                    last = nc.vector.bn_stats(bn1[par][:, a, :], h_all[:, b, a * D:(a + 1) * D])
                last.then_inc(dve_step, 1)

            def aggregate_1(par):
                for a in range(2):
                    last = nc.vector.bn_aggr(mv1[par][:, a, :], bn1[par][:, a, :])
                last.then_inc(stats1, 1)

            def norm_1(b, par):
                dve.wait_ge(rstd1_ready, b + 1)
                if not isinstance(b, int) or b >= 2:
                    dve.wait_ge(n1t_mm, b - 1)
                for a in range(2):
                    last = nc.vector.tensor_scalar(n1[par][:, a, :], h_all[:, b, a * D:(a + 1) * D],
                                                   mv1[par][:, a, 0:1], rstd1[par][:, a:a + 1],
                                                   ALU.subtract, ALU.mult)
                last.then_inc(n1_ready, 1)

            def row_max(b, par):
                dve.wait_ge(s_mm, b + 1)
                nc.vector.tensor_reduce(neg_max[par][:, :], s_ps, AX_X, ALU.max, negate=True).then_inc(max_ready, 1)

            def inverse_sums(b):
                dve.wait_ge(o_mm, b + 1)
                nc.vector.reciprocal(rinv[:, :], o_ps[:, :, D]).then_inc(dve_step, 1)

            def residual(b, n):
                dve.wait_ge(dve_step, n)
                nc.vector.tensor_tensor(rinv_keep[:, :], rinv[:, :], keep[:, :], ALU.mult).then_inc(dve_step, 1)
                dve.wait_ge(dve_step, n + 1)
                for a in range(2):
                    h = h_all[:, b, a * D:(a + 1) * D]
                    last = nc.vector.scalar_tensor_tensor(h, o_ps[:, a, 0:D], rinv_keep[:, a:a + 1], h,
                                                          ALU.mult, ALU.add)
                last.then_inc(resid_ready, 1)

            dve.wait_ge(rows_mm, 1)
            nc.vector.tensor_copy(gamma[:, :], bank_misc[0:H, 0:D]).then_inc(rows_ready, 1)
            for a in range(2):
                nc.vector.tensor_copy(beta2[:, a, :], bank_misc[0:H, D:2 * D])
            nc.vector.tensor_copy(b2_2[:, 0, :], bank_misc[0:H, 2 * D:3 * D]).then_inc(rows_ready, 1)
            nc.vector.tensor_copy(b2_2[:, 1, :], bank_misc[0:H, 2 * D:3 * D]).then_inc(rows_ready, 1)
            dve.wait_ge(rows_ready, 3)

            n = count["n"]

            def stats_1_alone(b, par, n):
                stats_1(b, par)
                dve.wait_ge(dve_step, n)
                aggregate_1(par)

            scale_x(0, 0)
            scale_x(1, 1)
            n += 1; stats_1_alone(0, 0, n)
            norm_1(0, 0)
            n += 1; stats_1_alone(1, 1, n)
            norm_1(1, 1)
            scale_x(2, 0)
            row_max(0, 0)
            nc.vector.tensor_reduce(row_sum[:, :], s_ps, AX_X, ALU.add).then_inc(sums_read, 1)
            n += 1; stats_1_alone(2, 0, n)
            norm_1(2, 0)
            scale_x(3, 1)
            dve.wait_ge(sums_t, 1)
            count["n"] = n
            chain(nc.vector.tensor_copy(sum_row[:, :], bank_misc[0:1, 0:T]))
            chain(nc.vector.tensor_reduce(least[:, :], sum_row[:, :], AX_X, ALU.min))
            chain(nc.vector.tensor_scalar(cand0[:, :], sum_row[:, :], least[:, :], BIG, ALU.is_gt, ALU.mult))
            dve.wait_ge(consts_ready, N_CONSTS)
            chain(nc.vector.tensor_tensor(cand[:, :], cand0[:, :], token_row[:, :], ALU.add))
            nc.vector.tensor_reduce(c0[:, :], cand[:, :], AX_X, ALU.min).then_inc(c0_ready, 1)
            dve.wait_ge(c0_bcast, 1)
            chain(nc.vector.tensor_copy(c0_col[:, :], bank_misc[0:H, 0:1]))
            dve.wait_ge(dve_consts, 1)
            chain(nc.vector.tensor_scalar(keep[:, :], token_col[:, :], c0_col[:, :], None, ALU.not_equal))
            n_loop = count["n"]

            with dve.Fori(1, NP - 1) as k:
                for par in range(2):
                    b = 2 * k + par
                    at = (k - 1) * 6 + (n_loop + 3 * par)
                    row_max(b - 1, 1 - par)
                    stats_1(b + 1, 1 - par)
                    dve.wait_ge(dve_step, at + 1)
                    inverse_sums(b - 2)
                    aggregate_1(1 - par)
                    residual(b - 2, at + 2)
                    norm_1(b + 1, 1 - par)
                    scale_x(b + 2, par)
            n = n_loop + 6 * (NP - 2)
            row_max(NB - 3, 1)
            n += 1; stats_1_alone(NB - 1, 1, n)
            inverse_sums(NB - 4)
            residual(NB - 4, n + 1); n += 2
            norm_1(NB - 1, 1)
            row_max(NB - 2, 0)
            inverse_sums(NB - 3)
            residual(NB - 3, n + 1); n += 2
            row_max(NB - 1, 1)
            inverse_sums(NB - 2)
            residual(NB - 2, n + 1); n += 2

            def tile2(j, t):
                return h_all[:, 2 * j + t // 2, (t % 2) * D:(t % 2 + 1) * D]

            def stats_2(j, par):
                dve.wait_ge(resid_ready, 2 * j + 2)
                for t in range(4):
                    last = nc.vector.bn_stats(bn2[par][:, t, :], tile2(j, t))
                last.then_inc(dve_step, 1)

            def aggregate_2(par):
                for t in range(4):
                    last = nc.vector.bn_aggr(mv2[par][:, t, :], bn2[par][:, t, :])
                last.then_inc(stats2, 1)

            def norm_2(j, par):
                dve.wait_ge(rstd2_ready, j + 1)
                if not isinstance(j, int) or j >= 2:
                    dve.wait_ge(t2_mm, j - 1)
                for t in range(4):
                    last = nc.vector.tensor_scalar(n2[par][:, t, :], tile2(j, t), mv2[par][:, t, 0:1],
                                                   rstd2[par][:, t:t + 1], ALU.subtract, ALU.mult)
                last.then_inc(n2_ready, 1)

            def finish(j, par):
                dve.wait_ge(y_mm, j + 1)
                dve.wait_ge(hb_ready, 2 * j + 2)
                nc.vector.tensor_tensor(hb_pairs[:, j, :], y_ps[par].rearrange("p n d -> p (n d)"),
                                        hb_pairs[:, j, :],
                                        ALU.add).then_inc(y_ready, 1)

            def stats_2_alone(j, par, n):
                stats_2(j, par)
                dve.wait_ge(dve_step, n)
                aggregate_2(par)

            n += 1; stats_2_alone(0, 0, n)
            n += 1; stats_2_alone(1, 1, n)
            norm_2(0, 0)
            norm_2(1, 1)
            inverse_sums(NB - 1)
            residual(NB - 1, n + 1); n += 2
            n += 1; stats_2_alone(2, 0, n)
            n += 1; stats_2_alone(3, 1, n)
            norm_2(2, 0)
            finish(0, 0)
            n_ff = n
            with dve.Fori(0, NP // 2 - 2) as m:
                for par in (1, 0):
                    j = 2 * m + (2 - par)
                    norm_2(j + 2, par)
                    stats_2(j + 3, 1 - par)
                    dve.wait_ge(dve_step, 2 * m + (2 - par + n_ff))
                    finish(j, par)
                    aggregate_2(1 - par)
            norm_2(NP - 1, 1)
            finish(NP - 3, 1)
            finish(NP - 2, 0)
            finish(NP - 1, 1)


def kernel(x, L0_tok_conv_w, L0_tok_conv_b, L0_tok_lin_w, L0_tok_lin_b, L0_tok_emb, L0_tok_ln_g, L0_tok_ln_b,
           L0_attn_kernel, L0_ffn_W1, L0_ffn_b1, L0_ffn_W2, L0_ffn_b2):
    import numpy as np
    import concourse.bacc as bacc
    from concourse.bass_utils import run_bass_kernel_spmd

    tok = np.concatenate([L0_tok_lin_w.T, L0_tok_conv_w[:, 0, :], L0_tok_conv_b[:, None]], axis=1)
    arrays = {
        "x_dram": np.ascontiguousarray(x),
        "tok_dram": np.ascontiguousarray(np.concatenate([tok, tok], axis=0)),
        "emb_dram": np.ascontiguousarray(np.concatenate([L0_tok_emb, L0_tok_lin_b[None, :]], axis=0)),
        "weights_dram": np.ascontiguousarray(np.concatenate(
            [L0_attn_kernel[0].T, L0_attn_kernel[1].T, L0_attn_kernel[2], L0_ffn_W1.T, L0_ffn_W2.T,
             L0_ffn_b1[:, None]], axis=1)),
        "rows_dram": np.ascontiguousarray(np.concatenate([L0_tok_ln_g, L0_tok_ln_b, L0_ffn_b2])[None, :]),
    }
    nc = bacc.Bacc("TRN2", target_bir_lowering=False, num_devices=1)
    args = [nc.dram_tensor(n, a.shape, mybir.dt.from_np(a.dtype), kind="ExternalInput").ap()
            for n, a in arrays.items()]
    out_shape = (x.shape[0], x.shape[2], L0_tok_lin_w.shape[0])
    args.append(nc.dram_tensor("out_dram", out_shape, F32, kind="ExternalOutput").ap())
    audio_tower(nc, *args)
    r = run_bass_kernel_spmd(nc, [arrays], core_ids=[0])
    return r.results[0]["out_dram"]
```

```python
from contextlib import ExitStack

import concourse.bass as bass
from concourse import mybir

ALU = mybir.AluOpType
ACT = mybir.ActivationFunctionType
AX_X = mybir.AxisListType.X
F32 = mybir.dt.float32
BF16 = mybir.dt.bfloat16

EPS = 1e-5
SCORE_SCALE = 1.0 / 64 ** 0.5


def audio_tower(nc, x, tok_pack, emb_pack, weights, rows, out):
    NB, C, T = x.shape
    D = out.shape[2]
    H = T // 2
    NP = NB // 2
    DV = D + 1
    BIG = float(4 * T)

    x_pairs = x.rearrange("(k h) c t -> k (h c) t", h=2)
    out_pairs = out.rearrange("(j b) (a p) d -> j p (b a) d", b=2, p=H)

    with ExitStack() as ctx:
        def sb(name, shape, dt=F32):
            return ctx.enter_context(nc.sbuf_tensor(name, shape, dt))

        def sem(name):
            return ctx.enter_context(nc.semaphore(name))

        def bank(name):
            return ctx.enter_context(nc.psum_tensor(name, [128, 512], F32))

        bank_x = [bank("bank_x0"), bank("bank_x1")]
        bank_np, bank_v, bank_s, bank_at, bank_o, bank_misc = (
            bank("bank_" + n) for n in ("np", "v", "s", "at", "o", "misc"))
        x_ps = [t[0:H, 0:2 * D].rearrange("p (a d) -> p a d", a=2) for t in bank_x]
        n1t_ps = bank_np[:, 0:T]
        p_ps = bank_np[:, 0:T]
        v_ps = bank_v[0:H, 0:2 * D].rearrange("p (a d) -> p a d", a=2)
        s_ps = bank_s[0:H, 0:2 * T].rearrange("p (a t) -> p a t", a=2)
        at_ps = bank_at[0:H, 0:2 * T].rearrange("p (c s) -> p c s", c=2)
        o_ps = bank_o[0:H, 0:2 * (D + 2)].rearrange("p (a d) -> p a d", a=2)
        t2_ps = [t[:, 0:2 * T] for t in bank_x]
        f1_ps = [bank_misc[:, 0:2 * T], bank_v[:, 0:2 * T]]
        y_ps = [t[0:H, :].rearrange("p (n d) -> p n d", d=D) for t in (bank_np, bank_at)]

        tok_w = sb("tok_w", [128, D + 4])
        lin_t = tok_w[:, 0:D]
        conv_b = tok_w[:, D + 3:D + 4]
        lin_c = sb("lin_c", [128, D])
        lin_mean = sb("lin_mean", [128, 1])
        emb_b = sb("emb_b", [C + 1, D])
        mean_w = sb("mean_w", [C + 1, C + 1])
        cb = sb("cb", [C + 1, D])
        cb_sum = sb("cb_sum", [C + 1, 1])
        cb_mean = sb("cb_mean", [C + 1, 1])
        cb_rest = sb("cb_rest", [C + 1, D])
        cb_rest2 = sb("cb_rest2", [C + 1, D])
        cb_hi = sb("cb_hi", [C + 1, D], BF16)
        cb_mid = sb("cb_mid", [C + 1, D], BF16)
        cb_rows = sb("cb_rows", [C + 1, D], BF16)
        ones_b = sb("ones_b", [C + 1, H], BF16)
        w_sb = sb("w_sb", [128, 5 * D + 1])
        wq_t, wk_t, w_v, w1_t, w2_t = (w_sb[:, n * D:(n + 1) * D] for n in range(5))
        b1_col = w_sb[:, 5 * D:5 * D + 1]
        qk_w = sb("qk_w", [128, D])
        rows_sb = sb("rows_sb", [1, 3 * D])
        ones_row = sb("ones_row", [1, H])
        gamma = sb("gamma", [H, D])
        beta4 = sb("beta4", [H, 4, D])
        b2_4 = sb("b2_4", [H, 4, D])
        ident = sb("ident", [128, 128])
        neg_half = sb("neg_half", [H, 4])
        eps = sb("eps", [H, 4])
        neg_one = sb("neg_one", [H, 4])
        one = sb("one", [H, 4])
        token_row = sb("token_row", [1, T])
        token_col = sb("token_col", [H, 2])

        x_slot = sb("x_slot", [128, T + 2])
        tap0 = sb("tap0", [128, T])
        tap01 = sb("tap01", [128, T])
        xc = sb("xc", [128, T])
        squared = sb("squared", [H, 4, D])
        var_x = sb("var_x", [H, 4])
        var_x_eps = sb("var_x_eps", [H, 4])
        rstd_x = sb("rstd_x", [H, 4])
        scaled = sb("scaled", [H, 4, D])
        h_all = sb("h_all", [H, NB, 2 * D])
        h_pairs = h_all[:, :, :].rearrange("p (k b) d -> p k (b d)", b=2)
        hb_all = sb("hb_all", [H, NP, 4 * D])
        bn1 = sb("bn1", [H, 4, 6])
        mv1 = sb("mv1", [H, 4, 2])
        var1_eps = sb("var1_eps", [H, 4])
        neg_mean1 = sb("neg_mean1", [H, 4])
        rstd1 = sb("rstd1", [H, 4])
        shift1 = sb("shift1", [H, 4])
        n1 = [sb(f"n1_{p}", [H, 2, D]) for p in range(2)]
        n1t = [sb(f"n1t{p}", [128, T]) for p in range(2)]
        pt = [sb(f"pt{p}", [128, T]) for p in range(2)]
        v_sb = [sb(f"v{p}", [H, 2, DV]) for p in range(2)]
        neg_max = [sb(f"neg_max{p}", [H, 2]) for p in range(2)]
        a_sb = [sb(f"a{p}", [H, 2, T]) for p in range(2)]
        at_sb = [sb(f"at{p}", [H, 2, T]) for p in range(2)]
        row_sum = sb("row_sum", [H, 2])
        sum_row = sb("sum_row", [1, T])
        least = sb("least", [1, 1])
        cand0 = sb("cand0", [1, T])
        cand = sb("cand", [1, T])
        c0 = sb("c0", [1, 1])
        c0_col = sb("c0_col", [H, 1])
        keep = sb("keep", [H, 2])
        rinv = sb("rinv", [H, 2])
        rinv_keep = sb("rinv_keep", [H, 2])
        bn2 = sb("bn2", [H, 4, 6])
        mv2 = sb("mv2", [H, 4, 2])
        var2_eps = sb("var2_eps", [H, 4])
        mean2 = sb("mean2", [H, NP, 4])
        rstd2 = sb("rstd2", [H, NP, 4])
        n2 = [sb(f"n2_{p}", [H, 4, D]) for p in range(2)]
        n2t = [sb(f"n2t{p}", [128, 2 * T]) for p in range(2)]
        g_sb = [sb(f"g{p}", [128, 2 * T]) for p in range(2)]

        landed_x, landed_tok, landed_emb, landed_w, landed_rows, out_done = (
            sem(n) for n in ("landed_x", "landed_tok", "landed_emb", "landed_w", "landed_rows", "out_done"))
        pad_zeroed, roots_consts, ident_zeroed, ident_ready, ones_ready, v_ones, iota_ready, tri_ready = (
            sem(n) for n in ("pad_zeroed", "roots_consts", "ident_zeroed", "ident_ready", "ones_ready",
                             "v_ones", "iota_ready", "tri_ready"))
        mean_w_ready, lin_centred, cb_mm, cb_ready, setup_step = (
            sem(n) for n in ("mean_w_ready", "lin_centred", "cb_mm", "cb_ready", "setup_step"))
        qk_mm, qk_ready, rows_mm, gamma_ready, rows_spread = (
            sem(n) for n in ("qk_mm", "qk_ready", "rows_mm", "gamma_ready", "rows_spread"))
        tap0_ready, tap01_ready, conv_ready, xvar_ready, xvar_eps_ready, rstd_x_ready, x_scaled, h_ready = (
            sem(n) for n in ("tap0_ready", "tap01_ready", "conv_ready", "xvar_ready", "xvar_eps_ready",
                             "rstd_x_ready", "x_scaled", "h_ready"))
        bn1_ready, stats1, eps1_ready, negm1_ready, rstd1_ready, shift1_ready, hb_ready = (
            sem(n) for n in ("bn1_ready", "stats1", "eps1_ready", "negm1_ready", "rstd1_ready",
                             "shift1_ready", "hb_ready"))
        bn2_ready, stats2, eps2_ready, mean2_ready, rstd2_ready = (
            sem(n) for n in ("bn2_ready", "stats2", "eps2_ready", "mean2_ready", "rstd2_ready"))
        n2_ready, t2_mm, n2t_ready, f1_mm, gelu_ready, y_mm, y_ready = (
            sem(n) for n in ("n2_ready", "t2_mm", "n2t_ready", "f1_mm", "gelu_ready", "y_mm", "y_ready"))
        x_mm, n1_ready, n1t_mm, n1t_ready, p_mm, p_ready, v_mm, v_ready = (
            sem(n) for n in ("x_mm", "n1_ready", "n1t_mm", "n1t_ready", "p_mm", "p_ready", "v_mm", "v_ready"))
        s_mm, max_ready, exp_ready, at_mm, at_ready, o_mm, rinv_ready, keep_applied, resid_ready = (
            sem(n) for n in ("s_mm", "max_ready", "exp_ready", "at_mm", "at_ready", "o_mm", "rinv_ready",
                             "keep_applied", "resid_ready"))
        sums_read, sums_turned, c0_ready, c0_spread = (
            sem(n) for n in ("sums_read", "sums_turned", "c0_ready", "c0_spread"))

        def after(value, first):
            return not isinstance(value, int) or value >= first

        block = ctx.enter_context(nc.Block())

        @block.sync
        def _(sp):
            sp.dma_start(x_slot[:, 1:T + 1], x_pairs[0]).then_inc(landed_x, 16)
            sp.dma_start(w_sb[:, :], weights).then_inc(landed_w, 16)
            with sp.Fori(1, NP) as k:
                sp.wait_ge(conv_ready, k)
                sp.dma_start(x_slot[:, 1:T + 1], x_pairs[k]).then_inc(landed_x, 16)
            with sp.Fori(0, NP) as j:
                sp.wait_ge(y_ready, j + 1)
                sp.dma_start(out_pairs[j], hb_all[:, j, :].rearrange("p (n d) -> p n d", d=D))\
                    .then_inc(out_done, 16)
            sp.wait_ge(out_done, 16 * NP)

        @block.gpsimd
        def _(pool):
            def first_tap(k):
                pool.tensor_scalar(tap0[:, :], x_slot[:, 0:T], tok_w[:, D:D + 1], conv_b,
                                   ALU.mult, ALU.add).then_inc(tap0_ready, 1)

            def root_x(k):
                pool.wait_ge(xvar_ready, 4 * k + 4)
                pool.tensor_tensor(var_x_eps[:, :], var_x[:, :], eps[:, :], ALU.add).then_inc(xvar_eps_ready, 1)
                pool.wait_ge(xvar_eps_ready, k + 1)
                pool.tensor_tensor(rstd_x[:, :], var_x_eps[:, :], neg_half[:, :], ALU.pow).then_inc(rstd_x_ready, 1)

            def root_1(k):
                pool.wait_ge(stats1, k + 1)
                pool.tensor_tensor(var1_eps[:, :], mv1[:, :, 1], eps[:, :], ALU.add).then_inc(eps1_ready, 1)
                pool.tensor_tensor(neg_mean1[:, :], mv1[:, :, 0], neg_one[:, :], ALU.mult).then_inc(negm1_ready, 1)
                pool.wait_ge(eps1_ready, k + 1)
                pool.tensor_tensor(rstd1[:, :], var1_eps[:, :], neg_half[:, :], ALU.pow).then_inc(rstd1_ready, 1)
                pool.wait_ge(negm1_ready, k + 1)
                pool.wait_ge(rstd1_ready, k + 1)
                pool.tensor_tensor(shift1[:, :], neg_mean1[:, :], rstd1[:, :], ALU.mult).then_inc(shift1_ready, 1)

            def root_2(k):
                pool.wait_ge(stats2, k + 1)
                pool.tensor_tensor(var2_eps[:, :], mv2[:, :, 1], eps[:, :], ALU.add).then_inc(eps2_ready, 1)
                pool.tensor_tensor(mean2[:, k, :], mv2[:, :, 0], one[:, :], ALU.mult).then_inc(mean2_ready, 1)
                pool.wait_ge(eps2_ready, k + 1)
                pool.tensor_tensor(rstd2[:, k, :], var2_eps[:, :], neg_half[:, :], ALU.pow).then_inc(rstd2_ready, 1)

            def add_beta(k):
                pool.wait_ge(x_scaled, k + 1)
                pool.tensor_tensor(h_pairs[:, k, :], scaled[:, :, :].rearrange("p n d -> p (n d)"),
                                   beta4[:, :, :].rearrange("p n d -> p (n d)"), ALU.add).then_inc(h_ready, 1)

            def add_b2(k):
                pool.wait_ge(resid_ready, 2 * k + 2)
                pool.tensor_tensor(hb_all[:, k, :], h_pairs[:, k, :],
                                   b2_4[:, :, :].rearrange("p n d -> p (n d)"), ALU.add).then_inc(hb_ready, 1)

            pool.memset(x_slot[:, 0:1], 0.0).then_inc(pad_zeroed, 1)
            pool.memset(x_slot[:, T + 1:T + 2], 0.0).then_inc(pad_zeroed, 1)
            pool.memset(ones_b[:, :], 1.0).then_inc(ones_ready, 1)
            pool.memset(ones_row[:, :], 1.0).then_inc(ones_ready, 1)
            pool.memset(neg_half[:, :], -0.5).then_inc(roots_consts, 1)
            pool.memset(eps[:, :], EPS).then_inc(roots_consts, 1)
            pool.memset(neg_one[:, :], -1.0).then_inc(roots_consts, 1)
            pool.memset(one[:, :], 1.0).then_inc(roots_consts, 1)
            pool.memset(ident[:, :], 0.0).then_inc(ident_zeroed, 1)
            pool.wait_ge(pad_zeroed, 2)
            pool.wait_ge(landed_tok, 16)
            pool.wait_ge(landed_x, 16)
            first_tap(0)
            pool.wait_ge(ident_zeroed, 1)
            pool.affine_select(out=ident[:, :], in_=ident[:, :], compare_op=ALU.not_equal, fill=1.0,
                               base=0, pattern=[[-1, 128]], channel_multiplier=1).then_inc(ident_ready, 1)
            for p in range(2):
                pool.memset(v_sb[p][:, :, D:DV], 1.0).then_inc(v_ones, 1)
            pool.iota(token_row[:, :], pattern=[[1, T]], base=0, channel_multiplier=0,
                      allow_small_or_imprecise_dtypes=True).then_inc(iota_ready, 1)
            pool.iota(token_col[:, :], pattern=[[H, 2]], base=0, channel_multiplier=1,
                      allow_small_or_imprecise_dtypes=True).then_inc(iota_ready, 1)
            pool.wait_ge(tap01_ready, 1)
            pool.wait_ge(landed_x, 32)
            first_tap(1)
            pool.wait_ge(roots_consts, 4)
            root_x(0)
            pool.wait_ge(rows_spread, 8)
            add_beta(0)
            pool.wait_ge(tap01_ready, 2)
            pool.wait_ge(landed_x, 48)
            first_tap(2)
            root_x(1)
            root_1(0)
            pool.wait_ge(landed_w, 16)
            for w in (w1_t, w2_t):
                pool.affine_select(out=w, in_=w, compare_op=ALU.is_ge, fill=0.0, base=0,
                                   pattern=[[1, D]], channel_multiplier=-1).then_inc(tri_ready, 1)
            add_beta(1)

            pool.wait_ge(landed_x, 64)
            pool.wait_ge(tap01_ready, 3)
            first_tap(3)
            root_1(1)
            root_x(2)
            add_beta(2)
            pool.wait_ge(landed_x, 80)
            first_tap(4)
            with pool.Fori(1, NP - 4) as k:
                root_1(k + 1)
                root_x(k + 2)
                pool.wait_ge(landed_x, 16 * (k + 5))
                pool.wait_ge(tap01_ready, k + 4)
                add_beta(k + 2)
                first_tap(k + 4)
                root_2(k - 1)
                add_b2(k - 1)
            for k in range(NP - 4, NP - 2):
                root_1(k + 1)
                root_x(k + 2)
                add_beta(k + 2)
                root_2(k - 1)
                add_b2(k - 1)
            root_1(NP - 1)
            for k in range(NP - 3, NP):
                root_2(k)
                add_b2(k)

        @block.tensor
        def _(pe):
            def turn_n1(b, par):
                pe.wait_ge(n1_ready, b + 1)
                if after(b, 1):
                    pe.wait_ge(p_ready, b)
                for a in range(2):
                    last = nc.tensor.transpose(n1t_ps[:, a * H:(a + 1) * H], n1[par][:, a, :], ident[0:H, 0:H])
                last.then_inc(n1t_mm, 1)

            def queries(b, par):
                pe.wait_ge(n1t_ready, b + 1)
                nc.tensor.matmul(p_ps, qk_w[:, :], n1t[par][:, :], start=True, stop=True).then_inc(p_mm, 1)

            def values(b, par):
                if after(b, 1):
                    pe.wait_ge(v_ready, b)
                for a in range(2):
                    last = nc.tensor.matmul(v_ps[:, a, :], n1t[par][:, a * H:(a + 1) * H], w_v,
                                            start=True, stop=True)
                last.then_inc(v_mm, 1)

            def scores(b, par):
                pe.wait_ge(p_ready, b + 1)
                if after(b, 1):
                    pe.wait_ge(exp_ready, b)
                for a in range(2):
                    last = nc.tensor.matmul(s_ps[:, a, :], pt[par][:, a * H:(a + 1) * H], n1t[par][:, :],
                                            start=True, stop=True)
                last.then_inc(s_mm, 1)

            def turn_a(b, par):
                pe.wait_ge(exp_ready, b + 1)
                if after(b, 1):
                    pe.wait_ge(at_ready, b)
                for a in range(2):
                    for c in range(2):
                        last = nc.tensor.transpose(at_ps[:, c, a * H:(a + 1) * H],
                                                   a_sb[par][:, a, c * H:(c + 1) * H], ident[0:H, 0:H])
                last.then_inc(at_mm, 1)

            def attend(b, par):
                pe.wait_ge(at_ready, b + 1)
                pe.wait_ge(v_ready, b + 1)
                if after(b, 1):
                    pe.wait_ge(resid_ready, b)
                for a in range(2):
                    for c in range(2):
                        last = nc.tensor.matmul(o_ps[:, a, 0:DV], at_sb[par][:, c, a * H:(a + 1) * H],
                                                v_sb[par][:, c, :], start=(c == 0), stop=(c == 1))
                last.then_inc(o_mm, 1)

            def project_part(pair, par):
                if par == 0:
                    pe.wait_ge(conv_ready, pair + 1)
                    if after(pair, 1):
                        pe.wait_ge(x_scaled, pair)
                half = slice(par * C, (par + 1) * C)
                for a in range(2):
                    nc.tensor.matmul(x_ps[par][:, a, :], xc[half, a * H:(a + 1) * H], lin_c[half, :],
                                     start=True, stop=False)
                    last = nc.tensor.matmul(x_ps[par][:, a, :], ones_b[:, :], cb_rows[:, :],
                                            start=False, stop=True)
                last.then_inc(x_mm, 1)

            def step(b, par, pair=None, first=False):
                turn_n1(b, par)
                if pair is not None:
                    project_part(pair, par)
                queries(b, par)
                values(b, par)
                if not first:
                    turn_a(b - 1, 1 - par)
                scores(b, par)
                if not first:
                    attend(b - 1, 1 - par)

            pe.wait_ge(ones_ready, 2)
            pe.wait_ge(mean_w_ready, 2)
            pe.wait_ge(landed_emb, 16)
            nc.tensor.matmul(bank_misc[0:C + 1, 0:D], mean_w[:, :], emb_b[:, :], start=True, stop=True)\
                .then_inc(cb_mm, 1)
            pe.wait_ge(landed_rows, 16)
            nc.tensor.matmul(bank_s[0:H, 0:3 * D], ones_row[:, :], rows_sb[:, :], start=True, stop=True)\
                .then_inc(rows_mm, 1)
            pe.wait_ge(cb_ready, 3)
            pe.wait_ge(lin_centred, 1)
            project_part(0, 0)
            project_part(0, 1)
            pe.wait_ge(landed_w, 16)
            nc.tensor.matmul(bank_v[:, 0:D], wq_t, wk_t, start=True, stop=True).then_inc(qk_mm, 1)
            project_part(1, 0)
            project_part(1, 1)
            pe.wait_ge(qk_ready, 1)
            pe.wait_ge(rows_spread, 8)
            pe.wait_ge(gamma_ready, 1)
            pe.wait_ge(v_ones, 2)
            pe.wait_ge(ident_ready, 1)

            step(0, 0, pair=2, first=True)
            step(1, 1, pair=2)
            pe.wait_ge(sums_read, 1)
            for a in range(2):
                last = nc.tensor.transpose(bank_misc[0:1, a * H:(a + 1) * H], row_sum[:, a:a + 1], ident[0:H, 0:H])
            last.then_inc(sums_turned, 1)
            pe.wait_ge(c0_ready, 1)
            nc.tensor.matmul(bank_misc[0:H, 0:1], ones_row[:, :], c0[:, :], start=True, stop=True).then_inc(c0_spread, 1)

            with pe.Fori(1, NP - 2) as k:
                step(2 * k, 0, pair=k + 2)
                step(2 * k + 1, 1, pair=k + 2)
            for b in range(NB - 4, NB):
                step(b, b % 2)
            turn_a(NB - 1, 1)
            attend(NB - 1, 1)

            def turn_n2(j, par):
                pe.wait_ge(n2_ready, j + 1)
                if after(j, 2):
                    pe.wait_ge(n2t_ready, j - 1)
                for n in range(4):
                    last = nc.tensor.transpose(t2_ps[par][:, n * H:(n + 1) * H], n2[par][:, n, :], ident[0:H, 0:H])
                last.then_inc(t2_mm, 1)

            def up(j, par):
                pe.wait_ge(n2t_ready, j + 1)
                if after(j, 2):
                    pe.wait_ge(gelu_ready, j - 1)
                nc.tensor.matmul(f1_ps[par], w1_t, n2t[par][:, :], start=True, stop=True).then_inc(f1_mm, 1)

            def down(j, par):
                pe.wait_ge(gelu_ready, j + 1)
                for n in range(4):
                    last = nc.tensor.matmul(y_ps[par][:, n, :], g_sb[par][:, n * H:(n + 1) * H], w2_t,
                                            start=True, stop=True)
                last.then_inc(y_mm, 1)

            pe.wait_ge(tri_ready, 2)
            turn_n2(0, 0)
            turn_n2(1, 1)
            up(0, 0)
            turn_n2(2, 0)
            up(1, 1)
            down(0, 0)
            with pe.Fori(1, NP // 2 - 1) as m:
                for par in range(2):
                    turn_n2(2 * m + par + 1, 1 - par)
                    up(2 * m + par, par)
                    down(2 * m + par - 1, 1 - par)
            turn_n2(NP - 1, 1)
            up(NP - 2, 0)
            down(NP - 3, 1)
            up(NP - 1, 1)
            pe.wait_ge(y_ready, NP - 3)
            down(NP - 2, 0)
            pe.wait_ge(y_ready, NP - 2)
            down(NP - 1, 1)

        @block.scalar
        def _(act):
            act.dma_start(tok_w[:, :], tok_pack).then_inc(landed_tok, 16)
            act.dma_start(emb_b[:, :], emb_pack).then_inc(landed_emb, 16)
            act.dma_start(rows_sb[:, :], rows).then_inc(landed_rows, 16)

            def squares(pair):
                act.wait_ge(x_mm, 2 * pair + 2)
                for n in range(4):
                    nc.scalar.activation(squared[:, n, :], x_ps[n // 2][:, n % 2, :], ACT.Square, scale=float(D) ** -0.5,
                                         accum_out=var_x[:, n:n + 1]).then_inc(xvar_ready, 1)

            def normalize_1(pair, par):
                act.wait_ge(shift1_ready, pair + 1)
                if after(pair, 1):
                    act.wait_ge(n1t_mm, 2 * pair + par - 1)
                for a in range(2):
                    n = 2 * par + a
                    last = nc.scalar.activation(n1[par][:, a, :], h_pairs[:, pair, n * D:(n + 1) * D], ACT.Identity,
                                                bias=shift1[:, n:n + 1], scale=rstd1[:, n:n + 1])
                last.then_inc(n1_ready, 1)

            def out_n1t(b, par):
                act.wait_ge(n1t_mm, b + 1)
                if after(b, 2):
                    act.wait_ge(s_mm, b - 1)
                nc.scalar.activation(n1t[par][:, :], n1t_ps, ACT.Copy).then_inc(n1t_ready, 1)

            def out_p(b, par):
                act.wait_ge(p_mm, b + 1)
                nc.scalar.activation(pt[par][:, :], p_ps, ACT.Copy).then_inc(p_ready, 1)

            def out_v(b, par):
                act.wait_ge(v_mm, b + 1)
                if after(b, 2):
                    act.wait_ge(o_mm, b - 1)
                nc.scalar.activation(v_sb[par][:, :, 0:D], v_ps, ACT.Copy).then_inc(v_ready, 1)

            def exps(b, par):
                act.wait_ge(max_ready, b + 1)
                if isinstance(b, int) and b == 0:
                    act.wait_ge(sums_read, 1)
                for a in range(2):
                    last = nc.scalar.activation(a_sb[par][:, a, :], s_ps[:, a, :], ACT.Exp,
                                                bias=neg_max[par][:, a:a + 1])
                last.then_inc(exp_ready, 1)

            def out_at(b, par):
                act.wait_ge(at_mm, b + 1)
                nc.scalar.activation(at_sb[par][:, :, :], at_ps, ACT.Copy).then_inc(at_ready, 1)

            def step(k, norm=True, xs=True, first=False):
                out_n1t(2 * k, 0)
                if not first:
                    exps(2 * k - 1, 1)
                out_p(2 * k, 0)
                out_v(2 * k, 0)
                if not first:
                    out_at(2 * k - 1, 1)
                out_n1t(2 * k + 1, 1)
                exps(2 * k, 0)
                out_p(2 * k + 1, 1)
                if xs:
                    squares(k + 2)
                out_v(2 * k + 1, 1)
                out_at(2 * k, 0)
                if norm:
                    normalize_1(k + 1, 0)
                    normalize_1(k + 1, 1)

            squares(0)
            act.wait_ge(rows_mm, 1)
            for n in range(4):
                nc.scalar.activation(beta4[:, n, :], bank_s[0:H, D:2 * D], ACT.Copy).then_inc(rows_spread, 1)
            act.wait_ge(qk_mm, 1)
            nc.scalar.activation(qk_w[:, :], bank_v[:, 0:D], ACT.Copy, scale=SCORE_SCALE).then_inc(qk_ready, 1)
            act.wait_ge(gamma_ready, 1)
            for n in range(4):
                nc.scalar.activation(b2_4[:, n, :], bank_s[0:H, 2 * D:3 * D], ACT.Copy).then_inc(rows_spread, 1)
            act.wait_ge(x_scaled, 1)
            squares(1)
            normalize_1(0, 0)
            normalize_1(0, 1)
            step(0, first=True)
            with act.Fori(1, NP - 2) as k:
                step(k)
            step(NP - 2, xs=False)
            step(NP - 1, norm=False, xs=False)
            exps(NB - 1, 1)
            out_at(NB - 1, 1)

            def out_n2t(j, par):
                act.wait_ge(t2_mm, j + 1)
                if after(j, 2):
                    act.wait_ge(f1_mm, j - 1)
                nc.scalar.activation(n2t[par][:, :], t2_ps[par], ACT.Copy).then_inc(n2t_ready, 1)

            def gelu(j, par):
                act.wait_ge(f1_mm, j + 1)
                nc.scalar.activation(g_sb[par][:, :], f1_ps[par], ACT.Gelu, bias=b1_col).then_inc(gelu_ready, 1)

            out_n2t(0, 0)
            out_n2t(1, 1)
            gelu(0, 0)
            with act.Fori(1, NP // 2) as m:
                for par in (1, 0):
                    out_n2t(2 * m + 1 - par, 1 - par)
                    gelu(2 * m - par, par)
            gelu(NP - 1, 1)

        @block.vector
        def _(dve):
            steps = [0]

            def chain(ins):
                steps[0] += 1
                ins.then_inc(setup_step, 1)
                dve.wait_ge(setup_step, steps[0])

            def second_tap(k):
                nc.vector.scalar_tensor_tensor(tap01[:, :], x_slot[:, 1:T + 1], tok_w[:, D + 1:D + 2], tap0[:, :],
                                               ALU.mult, ALU.add).then_inc(tap01_ready, 1)

            def third_tap(k):
                dve.wait_ge(tap01_ready, k + 1)
                if after(k, 1):
                    dve.wait_ge(x_mm, 2 * k)
                nc.vector.scalar_tensor_tensor(xc[:, :], x_slot[:, 2:T + 2], tok_w[:, D + 2:D + 3], tap01[:, :],
                                               ALU.mult, ALU.add).then_inc(conv_ready, 1)

            def scale_x(k):
                dve.wait_ge(rstd_x_ready, k + 1)
                if after(k, 1):
                    dve.wait_ge(h_ready, k)
                for n in range(4):
                    last = nc.vector.scalar_tensor_tensor(scaled[:, n, :], x_ps[n // 2][:, n % 2, :], rstd_x[:, n:n + 1],
                                                          gamma[:, :], ALU.mult, ALU.mult)
                last.then_inc(x_scaled, 1)

            def stats_1(k):
                dve.wait_ge(h_ready, k + 1)
                for n in range(4):
                    last = nc.vector.bn_stats(bn1[:, n, :], h_pairs[:, k, n * D:(n + 1) * D])
                last.then_inc(bn1_ready, 1)

            def aggregate_1():
                for n in range(4):
                    last = nc.vector.bn_aggr(mv1[:, n, :], bn1[:, n, :])
                last.then_inc(stats1, 1)

            def row_max(b, par):
                dve.wait_ge(s_mm, b + 1)
                nc.vector.tensor_reduce(neg_max[par][:, :], s_ps, AX_X, ALU.max, negate=True).then_inc(max_ready, 1)

            def residual(b):
                dve.wait_ge(o_mm, b + 1)
                nc.vector.reciprocal(rinv[:, :], o_ps[:, :, D]).then_inc(rinv_ready, 1)
                dve.wait_ge(rinv_ready, b + 1)
                nc.vector.tensor_tensor(rinv_keep[:, :], rinv[:, :], keep[:, :], ALU.mult).then_inc(keep_applied, 1)
                dve.wait_ge(keep_applied, b + 1)
                for a in range(2):
                    h = h_all[:, b, a * D:(a + 1) * D]
                    last = nc.vector.scalar_tensor_tensor(h, o_ps[:, a, 0:D], rinv_keep[:, a:a + 1], h,
                                                          ALU.mult, ALU.add)
                last.then_inc(resid_ready, 1)

            def stats_2(k):
                dve.wait_ge(resid_ready, 2 * k + 2)
                for n in range(4):
                    last = nc.vector.bn_stats(bn2[:, n, :], h_pairs[:, k, n * D:(n + 1) * D])
                last.then_inc(bn2_ready, 1)

            def aggregate_2():
                for n in range(4):
                    last = nc.vector.bn_aggr(mv2[:, n, :], bn2[:, n, :])
                last.then_inc(stats2, 1)

            nc.vector.memset(mean_w[0:C, :], 1.0 / C).then_inc(mean_w_ready, 1)
            nc.vector.memset(mean_w[C:C + 1, :], 1.0).then_inc(mean_w_ready, 1)
            chain(nc.vector.memset(cb_rows[:, :], 0.0))
            dve.wait_ge(landed_tok, 16)
            chain(nc.vector.tensor_reduce(lin_mean[:, :], lin_t, AX_X, ALU.add))
            chain(nc.vector.tensor_scalar(lin_mean[:, :], lin_mean[:, :], 1.0 / D, None, ALU.mult))
            nc.vector.tensor_scalar(lin_c[:, :], lin_t, lin_mean[:, :], None, ALU.subtract).then_inc(lin_centred, 1)
            dve.wait_ge(tap0_ready, 1)
            second_tap(0)
            third_tap(0)
            dve.wait_ge(cb_mm, 1)
            chain(nc.vector.tensor_reduce(cb_sum[:, :], bank_misc[0:C + 1, 0:D], AX_X, ALU.add))
            chain(nc.vector.tensor_scalar(cb_mean[:, :], cb_sum[:, :], 1.0 / D, None, ALU.mult))
            chain(nc.vector.tensor_scalar(cb[:, :], bank_misc[0:C + 1, 0:D], cb_mean[:, :], None, ALU.subtract))
            chain(nc.vector.tensor_copy(cb_hi[:, :], cb[:, :]))
            chain(nc.vector.tensor_tensor(cb_rest[:, :], cb[:, :], cb_hi[:, :], ALU.subtract))
            chain(nc.vector.tensor_copy(cb_mid[:, :], cb_rest[:, :]))
            chain(nc.vector.tensor_tensor(cb_rest2[:, :], cb_rest[:, :], cb_mid[:, :], ALU.subtract))
            nc.vector.tensor_copy(cb_rows[0:1, :], cb_hi[0:1, :]).then_inc(cb_ready, 1)
            nc.vector.tensor_copy(cb_rows[32:33, :], cb_mid[32:33, :]).then_inc(cb_ready, 1)
            nc.vector.tensor_copy(cb_rows[64:65, :], cb_rest2[64:65, :]).then_inc(cb_ready, 1)
            dve.wait_ge(rows_mm, 1)
            dve.wait_ge(rows_spread, 4)
            chain(nc.vector.tensor_copy(gamma[:, :], bank_s[0:H, 0:D]))
            nc.vector.memset(cb_sum[:, :], 0.0).then_inc(gamma_ready, 1)

            dve.wait_ge(tap0_ready, 2)
            second_tap(1)
            third_tap(1)
            scale_x(0)
            stats_1(0)
            dve.wait_ge(bn1_ready, 1)
            aggregate_1()
            dve.wait_ge(tap0_ready, 3)
            second_tap(2)
            third_tap(2)
            scale_x(1)

            stats_1(1)
            dve.wait_ge(bn1_ready, 2)
            dve.wait_ge(n1_ready, 2)
            aggregate_1()
            dve.wait_ge(tap0_ready, 4)
            second_tap(3)
            row_max(0, 0)
            nc.vector.tensor_reduce(row_sum[:, :], s_ps, AX_X, ALU.add).then_inc(sums_read, 1)
            third_tap(3)
            scale_x(2)
            dve.wait_ge(sums_turned, 1)
            chain(nc.vector.tensor_copy(sum_row[:, :], bank_misc[0:1, 0:T]))
            chain(nc.vector.tensor_reduce(least[:, :], sum_row[:, :], AX_X, ALU.min))
            chain(nc.vector.tensor_scalar(cand0[:, :], sum_row[:, :], least[:, :], BIG, ALU.is_gt, ALU.mult))
            dve.wait_ge(iota_ready, 2)
            chain(nc.vector.tensor_tensor(cand[:, :], cand0[:, :], token_row[:, :], ALU.add))
            nc.vector.tensor_reduce(c0[:, :], cand[:, :], AX_X, ALU.min).then_inc(c0_ready, 1)
            dve.wait_ge(c0_spread, 1)
            chain(nc.vector.tensor_copy(c0_col[:, :], bank_misc[0:H, 0:1]))
            chain(nc.vector.tensor_scalar(keep[:, :], token_col[:, :], c0_col[:, :], None, ALU.not_equal))

            with dve.Fori(1, NP - 3) as k:
                row_max(2 * k - 1, 1)
                residual(2 * k - 2)
                stats_1(k + 1)
                dve.wait_ge(bn1_ready, k + 2)
                dve.wait_ge(n1_ready, 2 * k + 2)
                dve.wait_ge(tap0_ready, k + 4)
                second_tap(k + 3)
                aggregate_1()
                row_max(2 * k, 0)
                third_tap(k + 3)
                residual(2 * k - 1)
                stats_2(k - 1)
                dve.wait_ge(bn2_ready, k)
                scale_x(k + 2)
                aggregate_2()
            for k in range(NP - 3, NP):
                row_max(2 * k - 1, 1)
                residual(2 * k - 2)
                if k < NP - 1:
                    stats_1(k + 1)
                    dve.wait_ge(bn1_ready, k + 2)
                    dve.wait_ge(n1_ready, 2 * k + 2)
                    aggregate_1()
                row_max(2 * k, 0)
                residual(2 * k - 1)
                stats_2(k - 1)
                if k < NP - 2:
                    scale_x(k + 2)
                dve.wait_ge(bn2_ready, k)
                dve.wait_ge(rstd2_ready, k - 1)
                aggregate_2()
            row_max(NB - 1, 1)

            def finish(j, par):
                dve.wait_ge(y_mm, j + 1)
                dve.wait_ge(hb_ready, j + 1)
                nc.vector.tensor_tensor(hb_all[:, j, :], y_ps[par].rearrange("p n d -> p (n d)"), hb_all[:, j, :],
                                        ALU.add).then_inc(y_ready, 1)

            def normalize_2(j, par):
                dve.wait_ge(mean2_ready, j + 1)
                dve.wait_ge(rstd2_ready, j + 1)
                if after(j, 2):
                    dve.wait_ge(t2_mm, j - 1)
                for n in range(4):
                    last = nc.vector.tensor_scalar(n2[par][:, n, :], h_pairs[:, j, n * D:(n + 1) * D],
                                                   mean2[:, j, n:n + 1], rstd2[:, j, n:n + 1],
                                                   ALU.subtract, ALU.mult)
                last.then_inc(n2_ready, 1)

            residual(NB - 2)
            normalize_2(0, 0)
            residual(NB - 1)
            stats_2(NP - 1)
            normalize_2(1, 1)
            dve.wait_ge(bn2_ready, NP)
            dve.wait_ge(rstd2_ready, NP - 1)
            aggregate_2()
            normalize_2(2, 0)
            normalize_2(3, 1)
            finish(0, 0)
            with dve.Fori(1, NP // 2 - 1) as m:
                for par in (1, 0):
                    normalize_2(2 * m + 3 - par, 1 - par)
                    finish(2 * m - par, par)
            for j in range(NP - 3, NP):
                finish(j, j % 2)


def kernel(x, L0_tok_conv_w, L0_tok_conv_b, L0_tok_lin_w, L0_tok_lin_b, L0_tok_emb, L0_tok_ln_g, L0_tok_ln_b,
           L0_attn_kernel, L0_ffn_W1, L0_ffn_b1, L0_ffn_W2, L0_ffn_b2):
    import numpy as np
    import concourse.bacc as bacc
    from concourse.bass_utils import run_bass_kernel_spmd

    tok = np.concatenate([L0_tok_lin_w.T, L0_tok_conv_w[:, 0, :], L0_tok_conv_b[:, None]], axis=1)
    arrays = {
        "x_dram": np.ascontiguousarray(x),
        "tok_dram": np.ascontiguousarray(np.concatenate([tok, tok], axis=0)),
        "emb_dram": np.ascontiguousarray(np.concatenate([L0_tok_emb, L0_tok_lin_b[None, :]], axis=0)),
        "weights_dram": np.ascontiguousarray(np.concatenate(
            [L0_attn_kernel[0].T, L0_attn_kernel[1].T, L0_attn_kernel[2], L0_ffn_W1.T, L0_ffn_W2.T,
             L0_ffn_b1[:, None]], axis=1)),
        "rows_dram": np.ascontiguousarray(np.concatenate([L0_tok_ln_g, L0_tok_ln_b, L0_ffn_b2])[None, :]),
    }
    nc = bacc.Bacc("TRN2", target_bir_lowering=False, num_devices=1)
    args = [nc.dram_tensor(n, a.shape, mybir.dt.from_np(a.dtype), kind="ExternalInput").ap()
            for n, a in arrays.items()]
    out_shape = (x.shape[0], x.shape[2], L0_tok_lin_w.shape[0])
    args.append(nc.dram_tensor("out_dram", out_shape, F32, kind="ExternalOutput").ap())
    audio_tower(nc, *args)
    r = run_bass_kernel_spmd(nc, [arrays], core_ids=[0])
    return r.results[0]["out_dram"]
```

```python
from contextlib import ExitStack

import concourse.bass as bass
from concourse import mybir

ALU = mybir.AluOpType
ACT = mybir.ActivationFunctionType
AX_X = mybir.AxisListType.X
F32 = mybir.dt.float32
BF16 = mybir.dt.bfloat16

EPS = 1e-5
SCORE_SCALE = 1.0 / 64 ** 0.5


def audio_tower(nc, x, tok_pack, weights, rows, out):
    NB, C, T = x.shape
    D = out.shape[2]
    H = T // 2
    NP = NB // 2
    DV = D + 1
    BIG = float(4 * T)

    x_pairs = x.rearrange("(k h) c t -> k (h c) t", h=2)
    out_pairs = out.rearrange("(j b) (a p) d -> j p (b a) d", b=2, p=H)

    with ExitStack() as ctx:
        def sb(name, shape, dt=F32):
            return ctx.enter_context(nc.sbuf_tensor(name, shape, dt))

        def sem(name):
            return ctx.enter_context(nc.semaphore(name))

        def bank(name):
            return ctx.enter_context(nc.psum_tensor(name, [128, 512], F32))

        bank_x = [bank("bank_x0"), bank("bank_x1")]
        bank_np, bank_v, bank_s0, bank_s1, bank_at, bank_o = (
            bank("bank_" + n) for n in ("np", "v", "s0", "s1", "at", "o"))
        x_ps = [t[0:H, 0:2 * D].rearrange("p (a d) -> p a d", a=2) for t in bank_x]
        n1t_ps = bank_np[:, 0:T]
        p_ps = bank_np[:, 0:T]
        v_ps = bank_v[0:H, 0:2 * D].rearrange("p (a d) -> p a d", a=2)
        s_ps = [t[0:H, 0:2 * T].rearrange("p (a t) -> p a t", a=2) for t in (bank_s0, bank_s1)]
        at_ps = bank_at[0:H, 0:2 * T].rearrange("p (c s) -> p c s", c=2)
        o_ps = bank_o[0:H, 0:2 * (D + 2)].rearrange("p (a d) -> p a d", a=2)
        sums_ps = bank_v[0:H, 0:T]
        t2_ps = [t[:, 0:2 * T] for t in bank_x]
        f1_ps = [bank_s0[:, 0:2 * T], bank_v[:, 0:2 * T]]
        y_ps = [t[0:H, :].rearrange("p (n d) -> p n d", d=D) for t in (bank_np, bank_at)]
        y_last_ps = bank_x[0][0:H, :].rearrange("p (n d) -> p n d", d=D)

        tok_w = sb("tok_w", [128, 2 * D + 4])
        lin_t = tok_w[:, 0:D]
        emb_b = tok_w[:, D + 4:2 * D + 4]
        conv_b = tok_w[:, D + 3:D + 4]
        lin_c = sb("lin_c", [128, D])
        lin_mean = sb("lin_mean", [128, 1])
        emb_mean = sb("emb_mean", [128, 1])
        emb_c = sb("emb_c", [128, D])
        mean_w = sb("mean_w", [128, H])
        cb_all = sb("cb_all", [H, D])
        cb_rest = sb("cb_rest", [C + 1, D])
        cb_rest2 = sb("cb_rest2", [C + 1, D])
        cb_hi = sb("cb_hi", [C + 1, D], BF16)
        cb_mid = sb("cb_mid", [C + 1, D], BF16)
        cb_rows = sb("cb_rows", [C + 1, D], BF16)
        warm = sb("warm", [128, 64], BF16)
        ones_b = sb("ones_b", [C + 1, H], BF16)
        w_sb = sb("w_sb", [128, 5 * D + 1])
        wq_t, wk_t, w_v, w1_t, w2_t = (w_sb[:, n * D:(n + 1) * D] for n in range(5))
        b1_col = w_sb[:, 5 * D:5 * D + 1]
        qk_w = sb("qk_w", [128, D])
        rows_sb = sb("rows_sb", [H, 3 * D])
        gamma = rows_sb[:, 0:D]
        beta_4, b2_4 = (rows_sb[:, n * D:(n + 1) * D].unsqueeze(1).broadcast_to((H, 4, D)) for n in (1, 2))
        ones_f = sb("ones_f", [H, H])
        ident = sb("ident", [128, 128])
        neg_half = sb("neg_half", [H, 4])
        eps = sb("eps", [H, 4])
        neg_one = sb("neg_one", [H, 4])
        one = sb("one", [H, 4])
        token_row = sb("token_row", [H, T])
        token_col = sb("token_col", [H, 2])

        x_head = sb("x_head", [128, 4, T + 2])
        x_slot = sb("x_slot", [128, T + 2])
        tap0 = sb("tap0", [128, T])
        tap01 = sb("tap01", [128, T])
        xc = sb("xc", [128, T])
        x_first = [sb(f"x_first{p}", [H, 2, D]) for p in range(2)]
        squared = sb("squared", [H, 4, D])
        var_x = sb("var_x", [H, 4])
        var_x_eps = sb("var_x_eps", [H, 4])
        rstd_x = sb("rstd_x", [H, 4])
        scaled = sb("scaled", [H, 4, D])
        h_all = sb("h_all", [H, NB, 2 * D])
        h_pairs = h_all[:, :, :].rearrange("p (k b) d -> p k (b d)", b=2)
        h_tiles = h_all[:, :, :].rearrange("p (k b) (a d) -> p k (b a) d", b=2, a=2)
        hb_all = sb("hb_all", [H, NP, 4, D])
        bn1 = sb("bn1", [H, 4, 6])
        mv1 = sb("mv1", [H, 4, 2])
        var1_eps = sb("var1_eps", [H, 4])
        neg_mean1 = sb("neg_mean1", [H, 4])
        rstd1 = sb("rstd1", [H, 4])
        shift1 = sb("shift1", [H, 4])
        n1 = [sb(f"n1_{p}", [H, 2, D]) for p in range(2)]
        n1t = [sb(f"n1t{p}", [128, T]) for p in range(2)]
        pt = [sb(f"pt{p}", [128, T]) for p in range(2)]
        v_sb = [sb(f"v{p}", [H, 2, DV]) for p in range(2)]
        neg_max = [sb(f"neg_max{p}", [H, 2]) for p in range(2)]
        a_sb = [sb(f"a{p}", [H, 2, T]) for p in range(2)]
        at_sb = [sb(f"at{p}", [H, 2, T]) for p in range(2)]
        row_sum = sb("row_sum", [H, 2])
        sum_diag = sb("sum_diag", [H, T])
        least = sb("least", [H, 1])
        cand0 = sb("cand0", [H, T])
        cand = sb("cand", [H, T])
        c0 = sb("c0", [H, 1])
        keep = sb("keep", [H, 2])
        rinv = sb("rinv", [H, 2])
        rinv_keep = sb("rinv_keep", [H, 2])
        bn2 = sb("bn2", [H, 4, 6])
        mv2 = sb("mv2", [H, 4, 2])
        var2_eps = sb("var2_eps", [H, 4])
        mean2 = sb("mean2", [H, NP, 4])
        rstd2 = sb("rstd2", [H, NP, 4])
        n2 = [sb(f"n2_{p}", [H, 4, D]) for p in range(2)]
        n2t = [sb(f"n2t{p}", [128, 2 * T]) for p in range(2)]
        g_sb = [sb(f"g{p}", [128, 2 * T]) for p in range(2)]

        landed_head = [sem(f"landed_x{k}") for k in range(4)]
        landed_x, landed_tok, landed_w, landed_rows, out_done = (
            sem(n) for n in ("landed_x", "landed_tok", "landed_w", "landed_rows", "out_done"))
        pads_zeroed, roots_consts, ident_zeroed, ident_ready, ones_ready, v_ones, iota_ready, tri_ready = (
            sem(n) for n in ("pads_zeroed", "roots_consts", "ident_zeroed", "ident_ready", "ones_ready",
                             "v_ones", "iota_ready", "tri_ready"))
        mean_w_ready, lin_centred, emb_centred, cb_mm, cb_ready, setup_step, qk_mm, qk_ready = (
            sem(n) for n in ("mean_w_ready", "lin_centred", "emb_centred", "cb_mm", "cb_ready", "setup_step",
                             "qk_mm", "qk_ready"))
        means_step, warm_ready, cb_all_ready, x_first_ready = (
            sem(n) for n in ("means_step", "warm_ready", "cb_all_ready", "x_first_ready"))
        tap0_ready, tap01_ready, conv_ready = (
            sem(n) for n in ("tap0_ready", "tap01_ready", "conv_ready"))
        xvar_ready, xvar_eps_ready, rstd_x_ready, x_scaled, h_ready = (
            sem(n) for n in ("xvar_ready", "xvar_eps_ready",
                             "rstd_x_ready", "x_scaled", "h_ready"))
        bn1_ready, stats1, eps1_ready, negm1_ready, rstd1_ready, shift1_ready, hb_ready = (
            sem(n) for n in ("bn1_ready", "stats1", "eps1_ready", "negm1_ready", "rstd1_ready",
                             "shift1_ready", "hb_ready"))
        stats2, eps2_ready, mean2_ready, rstd2_ready = (
            sem(n) for n in ("stats2", "eps2_ready", "mean2_ready", "rstd2_ready"))
        n2_ready, t2_mm, n2t_ready, f1_mm, gelu_ready, y_mm, y_ready = (
            sem(n) for n in ("n2_ready", "t2_mm", "n2t_ready", "f1_mm", "gelu_ready", "y_mm", "y_ready"))
        x_mm, n1_ready, n1t_mm, n1t_ready, p_mm, p_ready, v_mm, v_ready = (
            sem(n) for n in ("x_mm", "n1_ready", "n1t_mm", "n1t_ready", "p_mm", "p_ready", "v_mm", "v_ready"))
        s_mm, max_ready, exp_ready, at_mm, at_ready, o_mm, rinv_ready, keep_applied, resid_ready, bn2_ready = (
            sem(n) for n in ("s_mm", "max_ready", "exp_ready", "at_mm", "at_ready", "o_mm", "rinv_ready",
                             "keep_applied", "resid_ready", "bn2_ready"))
        sums_diagonal, sums_spread, sums_used, keep_ready = (
            sem(n) for n in ("sums_diagonal", "sums_spread", "sums_used", "keep_ready"))

        def after(value, first):
            return not isinstance(value, int) or value >= first

        block = ctx.enter_context(nc.Block())

        @block.sync
        def _(sp):
            sp.dma_start(x_head[:, 0, 1:T + 1], x_pairs[0]).then_inc(landed_head[0], 16)
            sp.dma_start(x_head[:, 1, 1:T + 1], x_pairs[1]).then_inc(landed_head[1], 16)
            sp.dma_start(w_sb[:, :], weights).then_inc(landed_w, 16)
            sp.dma_start(x_head[:, 2, 1:T + 1], x_pairs[2]).then_inc(landed_head[2], 16)
            sp.dma_start(x_head[:, 3, 1:T + 1], x_pairs[3]).then_inc(landed_head[3], 16)
            sp.dma_start(x_slot[:, 1:T + 1], x_pairs[4]).then_inc(landed_x, 16)
            with sp.Fori(5, NP) as k:
                sp.wait_ge(conv_ready, k)
                sp.dma_start(x_slot[:, 1:T + 1], x_pairs[k]).then_inc(landed_x, 16)
            with sp.Fori(0, NP - 1) as j:
                sp.wait_ge(y_ready, 2 * j + 2)
                sp.dma_start(out_pairs[j], hb_all[:, j, :, :]).then_inc(out_done, 16)
            for b in (NB - 2, NB - 1):
                sp.wait_ge(y_ready, b + 1)
                tiles = slice(2 * (b % 2), 2 * (b % 2) + 2)
                sp.dma_start(out_pairs[NP - 1][:, tiles, :], hb_all[:, NP - 1, tiles, :]).then_inc(out_done, 16)
            sp.wait_ge(out_done, 16 * (NP + 1))

        @block.gpsimd
        def _(pool):
            def first_tap(src):
                pool.tensor_scalar(tap0[:, :], src[:, 0:T], tok_w[:, D:D + 1], conv_b,
                                   ALU.mult, ALU.add).then_inc(tap0_ready, 1)

            def root_x(pair, par=0, m=2):
                tiles, done = slice(2 * par, 2 * par + 2 * m), 2 * pair + par + m
                pool.wait_ge(xvar_ready, 2 * done)
                pool.tensor_tensor(var_x_eps[:, tiles], var_x[:, tiles], eps[:, tiles], ALU.add)\
                    .then_inc(xvar_eps_ready, m)
                pool.wait_ge(xvar_eps_ready, done)
                pool.tensor_tensor(rstd_x[:, tiles], var_x_eps[:, tiles], neg_half[:, tiles], ALU.pow)\
                    .then_inc(rstd_x_ready, m)

            def root_1(pair, par=0, m=2):
                tiles, done = slice(2 * par, 2 * par + 2 * m), 2 * pair + par + m
                pool.wait_ge(stats1, done)
                pool.tensor_tensor(var1_eps[:, tiles], mv1[:, tiles, 1], eps[:, tiles], ALU.add).then_inc(eps1_ready, m)
                if after(pair, 1):
                    pool.tensor_tensor(neg_mean1[:, tiles], mv1[:, tiles, 0], neg_one[:, tiles], ALU.mult)\
                        .then_inc(negm1_ready, m)
                pool.wait_ge(eps1_ready, done)
                if after(done, 3):
                    pool.wait_ge(n1_ready, done - 2)
                pool.tensor_tensor(rstd1[:, tiles], var1_eps[:, tiles], neg_half[:, tiles], ALU.pow)\
                    .then_inc(rstd1_ready, m)
                if after(pair, 1):
                    pool.wait_ge(negm1_ready, done - 2)
                    pool.wait_ge(rstd1_ready, done)
                    pool.tensor_tensor(shift1[:, tiles], neg_mean1[:, tiles], rstd1[:, tiles], ALU.mult)\
                        .then_inc(shift1_ready, m)

            def root_2(k):
                pool.wait_ge(stats2, k + 1)
                pool.tensor_tensor(var2_eps[:, :], mv2[:, :, 1], eps[:, :], ALU.add).then_inc(eps2_ready, 1)
                pool.tensor_tensor(mean2[:, k, :], mv2[:, :, 0], one[:, :], ALU.mult).then_inc(mean2_ready, 1)
                pool.wait_ge(eps2_ready, k + 1)
                pool.tensor_tensor(rstd2[:, k, :], var2_eps[:, :], neg_half[:, :], ALU.pow).then_inc(rstd2_ready, 1)

            def add_beta(k):
                pool.wait_ge(x_scaled, 2 * k + 2)
                pool.tensor_tensor(h_tiles[:, k, :, :], scaled[:, :, :], beta_4, ALU.add).then_inc(h_ready, 2)

            def add_b2(k):
                pool.wait_ge(resid_ready, 2 * k + 2)
                pool.tensor_tensor(hb_all[:, k, :, :], h_tiles[:, k, :, :], b2_4, ALU.add).then_inc(hb_ready, 1)

            pool.memset(x_head[:, :, 0:1], 0.0).then_inc(pads_zeroed, 1)
            pool.memset(x_head[:, :, T + 1:T + 2], 0.0).then_inc(pads_zeroed, 1)
            pool.memset(x_slot[:, 0:1], 0.0).then_inc(pads_zeroed, 1)
            pool.memset(x_slot[:, T + 1:T + 2], 0.0).then_inc(pads_zeroed, 1)
            pool.memset(neg_half[:, :], -0.5).then_inc(roots_consts, 1)
            pool.memset(eps[:, :], EPS).then_inc(roots_consts, 1)
            pool.memset(neg_one[:, :], -1.0).then_inc(roots_consts, 1)
            pool.memset(one[:, :], 1.0).then_inc(roots_consts, 1)
            pool.memset(ident[:, :], 0.0).then_inc(ident_zeroed, 1)
            for p in range(2):
                pool.memset(v_sb[p][:, :, D:DV], 1.0).then_inc(v_ones, 1)
            pool.wait_ge(ident_zeroed, 1)
            pool.affine_select(out=ident[:, :], in_=ident[:, :], compare_op=ALU.not_equal, fill=1.0,
                               base=0, pattern=[[-1, 128]], channel_multiplier=1).then_inc(ident_ready, 1)
            pool.wait_ge(pads_zeroed, 4)
            pool.wait_ge(landed_tok, 16)
            pool.wait_ge(landed_head[0], 16)
            first_tap(x_head[:, 0, :])
            pool.iota(token_row[:, :], pattern=[[1, T]], base=0, channel_multiplier=0,
                      allow_small_or_imprecise_dtypes=True).then_inc(iota_ready, 1)
            pool.iota(token_col[:, :], pattern=[[H, 2]], base=0, channel_multiplier=1,
                      allow_small_or_imprecise_dtypes=True).then_inc(iota_ready, 1)
            pool.wait_ge(tap01_ready, 1)
            pool.wait_ge(landed_head[1], 16)
            first_tap(x_head[:, 1, :])
            pool.wait_ge(roots_consts, 4)
            root_x(0, 0, 1)
            root_x(0, 1, 1)
            root_1(0, 0, 1)
            root_x(1, 0, 1)
            root_1(0, 1, 1)
            pool.wait_ge(tap01_ready, 2)
            pool.wait_ge(landed_head[2], 16)
            first_tap(x_head[:, 2, :])
            root_x(1, 1, 1)
            root_1(1, 0, 1)
            pool.wait_ge(landed_head[3], 16)
            pool.wait_ge(tap01_ready, 3)
            first_tap(x_head[:, 3, :])
            root_1(1, 1, 1)
            root_x(2)
            pool.wait_ge(landed_rows, 16)
            add_beta(2)
            pool.wait_ge(landed_x, 16)
            pool.wait_ge(tap01_ready, 4)
            first_tap(x_slot)
            pool.wait_ge(landed_w, 16)
            for w in (w1_t, w2_t):
                pool.affine_select(out=w, in_=w, compare_op=ALU.is_ge, fill=0.0, base=0,
                                   pattern=[[1, D]], channel_multiplier=-1).then_inc(tri_ready, 1)
            with pool.Fori(1, NP - 4) as k:
                root_1(k + 1)
                root_x(k + 2)
                pool.wait_ge(landed_x, 16 * k + 16)
                pool.wait_ge(tap01_ready, k + 4)
                add_beta(k + 2)
                first_tap(x_slot)
                root_2(k - 1)
            for k in range(NP - 4, NP - 2):
                root_1(k + 1)
                root_x(k + 2)
                add_beta(k + 2)
                root_2(k - 1)
            root_1(NP - 1)
            root_2(NP - 3)
            add_b2(0)
            add_b2(1)
            root_2(NP - 2)
            add_b2(2)
            root_2(NP - 1)
            with pool.Fori(3, NP) as k:
                add_b2(k)

        @block.tensor
        def _(pe):
            def turn_n1(b, par):
                pe.wait_ge(n1_ready, b + 1)
                for a in range(2):
                    last = nc.tensor.transpose(n1t_ps[:, a * H:(a + 1) * H], n1[par][:, a, :], ident[0:H, 0:H])
                last.then_inc(n1t_mm, 1)

            def queries(b, par):
                pe.wait_ge(n1t_ready, b + 1)
                nc.tensor.matmul(p_ps, qk_w[:, :], n1t[par][:, :], start=True, stop=True).then_inc(p_mm, 1)

            def values(b, par):
                for a in range(2):
                    last = nc.tensor.matmul(v_ps[:, a, :], n1t[par][:, a * H:(a + 1) * H], w_v,
                                            start=True, stop=True)
                last.then_inc(v_mm, 1)

            def scores(b, par):
                pe.wait_ge(p_ready, b + 1)
                for a in range(2):
                    last = nc.tensor.matmul(s_ps[par][:, a, :], pt[par][:, a * H:(a + 1) * H], n1t[par][:, :],
                                            start=True, stop=True)
                last.then_inc(s_mm, 1)

            def turn_a(b, par):
                pe.wait_ge(exp_ready, b + 1)
                for a in range(2):
                    for c in range(2):
                        last = nc.tensor.transpose(at_ps[:, c, a * H:(a + 1) * H],
                                                   a_sb[par][:, a, c * H:(c + 1) * H], ident[0:H, 0:H])
                last.then_inc(at_mm, 1)

            def attend(b, par):
                pe.wait_ge(at_ready, b + 1)
                if after(b, 1):
                    pe.wait_ge(resid_ready, b)
                for a in range(2):
                    for c in range(2):
                        last = nc.tensor.matmul(o_ps[:, a, 0:DV], at_sb[par][:, c, a * H:(a + 1) * H],
                                                v_sb[par][:, c, :], start=(c == 0), stop=(c == 1))
                last.then_inc(o_mm, 1)

            def project(pair):
                pe.wait_ge(conv_ready, pair + 1)
                for a in range(2):
                    for par in range(2):
                        half = slice(par * C, (par + 1) * C)
                        nc.tensor.matmul(x_ps[par][:, a, :], xc[half, a * H:(a + 1) * H], lin_c[half, :],
                                         start=True, stop=False)
                    for par in range(2):
                        last = nc.tensor.matmul(x_ps[par][:, a, :], ones_b[:, 0:H], cb_rows[:, :],
                                                start=False, stop=True)
                        if a == 1:
                            last.then_inc(x_mm, 1)

            def keep_warm(count):
                for _ in range(count):
                    nc.tensor.matmul(bank_o[0:64, :], warm[:, :], warm[:, :].unsqueeze(1).broadcast_to((128, 8, 64)),
                                     start=True, stop=True)

            pe.wait_ge(warm_ready, 1)
            keep_warm(9)
            pe.wait_ge(ones_ready, 2)
            pe.wait_ge(mean_w_ready, 2)
            pe.wait_ge(emb_centred, 1)
            nc.tensor.matmul(bank_s0[0:H, 0:D], mean_w[:, :], emb_c[:, :], start=True, stop=True)\
                .then_inc(cb_mm, 1)
            keep_warm(1)
            pe.wait_ge(lin_centred, 1)
            pe.wait_ge(conv_ready, 1)
            for par in range(2):
                half = slice(par * C, (par + 1) * C)
                for a in range(2):
                    last = nc.tensor.matmul(x_ps[par][:, a, :], xc[half, a * H:(a + 1) * H], lin_c[half, :],
                                            start=True, stop=True)
                last.then_inc(x_mm, 1)
            pe.wait_ge(landed_w, 16)
            nc.tensor.matmul(bank_v[:, 0:D], wq_t, wk_t, start=True, stop=True).then_inc(qk_mm, 1)
            keep_warm(5)
            pe.wait_ge(cb_ready, 3)
            pe.wait_ge(x_first_ready, 2)
            project(1)
            keep_warm(9)
            pe.wait_ge(ident_ready, 1)
            turn_n1(0, 0)
            pe.wait_ge(qk_ready, 1)
            queries(0, 0)
            values(0, 0)
            scores(0, 0)
            turn_n1(1, 1)
            queries(1, 1)
            values(1, 1)
            pe.wait_ge(x_scaled, 4)
            project(2)
            turn_a(0, 0)
            scores(1, 1)
            turn_n1(2, 0)
            pe.wait_ge(v_ready, 2)
            pe.wait_ge(sums_diagonal, 1)
            nc.tensor.matmul(sums_ps, ones_f[:, :], sum_diag[:, :], start=True, stop=True).then_inc(sums_spread, 1)
            pe.wait_ge(v_ones, 2)
            attend(0, 0)
            pe.wait_ge(sums_used, 1)

            with pe.Fori(1, NP - 2) as k:
                queries(2 * k, 0)
                values(2 * k, 0)
                pe.wait_ge(x_scaled, 2 * k + 4)
                project(k + 2)
                turn_a(2 * k - 1, 1)
                scores(2 * k, 0)
                turn_n1(2 * k + 1, 1)
                attend(2 * k - 1, 1)
                queries(2 * k + 1, 1)
                values(2 * k + 1, 1)
                turn_a(2 * k, 0)
                scores(2 * k + 1, 1)
                turn_n1(2 * k + 2, 0)
                attend(2 * k, 0)
            for b in range(NB - 4, NB - 1):
                queries(b, b % 2)
                values(b, b % 2)
                turn_a(b - 1, 1 - b % 2)
                scores(b, b % 2)
                turn_n1(b + 1, 1 - b % 2)
                attend(b - 1, 1 - b % 2)

            def turn_n2(j, par):
                pe.wait_ge(n2_ready, j + 1)
                if after(j, 2):
                    pe.wait_ge(n2t_ready, j - 1)
                for n in range(4):
                    last = nc.tensor.transpose(t2_ps[par][:, n * H:(n + 1) * H], n2[par][:, n, :], ident[0:H, 0:H])
                last.then_inc(t2_mm, 1)

            def up(j, par):
                pe.wait_ge(n2t_ready, j + 1)
                if after(j, 2):
                    pe.wait_ge(gelu_ready, j - 1)
                nc.tensor.matmul(f1_ps[par], w1_t, n2t[par][:, :], start=True, stop=True).then_inc(f1_mm, 1)

            def down(j, par, banks=None):
                pe.wait_ge(gelu_ready, j + 1)
                if after(j, 2):
                    pe.wait_ge(y_ready, 2 * j - 2)
                for n in range(4):
                    bank = banks[n // 2] if banks else y_ps[par]
                    last = nc.tensor.matmul(bank[:, n, :], g_sb[par][:, n * H:(n + 1) * H], w2_t,
                                            start=True, stop=True)
                    if n % 2:
                        last.then_inc(y_mm, 1)

            queries(NB - 1, 1)
            values(NB - 1, 1)
            turn_n2(0, 0)
            turn_a(NB - 2, 0)
            scores(NB - 1, 1)
            turn_n2(1, 1)
            attend(NB - 2, 0)
            pe.wait_ge(tri_ready, 2)
            up(0, 0)
            turn_a(NB - 1, 1)
            up(1, 1)
            attend(NB - 1, 1)
            turn_n2(2, 0)
            down(0, 0)
            turn_n2(3, 1)
            up(2, 0)
            down(1, 1)
            with pe.Fori(1, NP // 2 - 1) as m:
                turn_n2(2 * m + 2, 0)
                up(2 * m + 1, 1)
                down(2 * m, 0)
                turn_n2(2 * m + 3, 1)
                up(2 * m + 2, 0)
                down(2 * m + 1, 1)
            up(NP - 1, 1)
            down(NP - 2, 0)
            down(NP - 1, 1, (y_ps[1], y_last_ps))

        @block.scalar
        def _(act):
            act.dma_start(tok_w[:, :], tok_pack).then_inc(landed_tok, 16)
            act.dma_start(rows_sb[:, :], rows.broadcast_to((H, 3 * D))).then_inc(landed_rows, 16)

            def squares(n, src=x_ps):
                nc.scalar.activation(squared[:, n, :], src[n // 2][:, n % 2, :], ACT.Square, scale=float(D) ** -0.5,
                                     accum_out=var_x[:, n:n + 1]).then_inc(xvar_ready, 1)

            def normalize_1(pair, par):
                act.wait_ge(shift1_ready, 2 * pair - 1 + par)
                for a in range(2):
                    n = 2 * par + a
                    last = nc.scalar.activation(n1[par][:, a, :], h_pairs[:, pair, n * D:(n + 1) * D], ACT.Identity,
                                                bias=shift1[:, n:n + 1], scale=rstd1[:, n:n + 1])
                last.then_inc(n1_ready, 1)

            def out_n1t(b, par):
                act.wait_ge(n1t_mm, b + 1)
                nc.scalar.activation(n1t[par][:, :], n1t_ps, ACT.Copy).then_inc(n1t_ready, 1)

            def out_p(b, par):
                act.wait_ge(p_mm, b + 1)
                nc.scalar.activation(pt[par][:, :], p_ps, ACT.Copy).then_inc(p_ready, 1)

            def out_v(b, par):
                act.wait_ge(v_mm, b + 1)
                nc.scalar.activation(v_sb[par][:, :, 0:D], v_ps, ACT.Copy).then_inc(v_ready, 1)

            def exps(b, par):
                act.wait_ge(max_ready, b + 1)
                for a in range(2):
                    last = nc.scalar.activation(a_sb[par][:, a, :], s_ps[par][:, a, :], ACT.Exp,
                                                bias=neg_max[par][:, a:a + 1])
                last.then_inc(exp_ready, 1)

            def out_at(b, par):
                act.wait_ge(at_mm, b + 1)
                nc.scalar.activation(at_sb[par][:, :, :], at_ps, ACT.Copy).then_inc(at_ready, 1)

            def step(k, xs=True):
                normalize_1(k, 1)
                out_p(2 * k, 0)
                out_v(2 * k, 0)
                if xs:
                    act.wait_ge(x_mm, 2 * k + 6)
                    squares(0)
                    squares(1)
                out_at(2 * k - 1, 1)
                if xs:
                    squares(2)
                    squares(3)
                out_n1t(2 * k + 1, 1)
                exps(2 * k, 0)
                out_p(2 * k + 1, 1)
                normalize_1(k + 1, 0)
                out_at(2 * k, 0)
                out_v(2 * k + 1, 1)
                out_n1t(2 * k + 2, 0)
                exps(2 * k + 1, 1)

            def head_squares(b, par):
                act.wait_ge(x_mm, b + 1)
                act.wait_ge(xvar_eps_ready, b - 1)
                squares(2 * par)
                squares(2 * par + 1)

            for n in range(4):
                act.wait_ge(x_first_ready, n // 2 + 1)
                squares(n, x_first)
            act.wait_ge(qk_mm, 1)
            nc.scalar.activation(qk_w[:, :], bank_v[:, 0:D], ACT.Copy, scale=SCORE_SCALE).then_inc(qk_ready, 1)
            head_squares(2, 0)
            head_squares(3, 1)
            out_n1t(0, 0)
            out_p(0, 0)
            out_v(0, 0)
            out_n1t(1, 1)
            out_p(1, 1)
            exps(0, 0)
            out_v(1, 1)
            normalize_1(1, 0)
            act.wait_ge(x_mm, 6)
            squares(0)
            squares(1)
            out_at(0, 0)
            squares(2)
            squares(3)
            out_n1t(2, 0)
            exps(1, 1)
            with act.Fori(1, NP - 2) as k:
                step(k)
            step(NP - 2, xs=False)

            def out_n2t(j, par):
                act.wait_ge(t2_mm, j + 1)
                if after(j, 2):
                    act.wait_ge(f1_mm, j - 1)
                nc.scalar.activation(n2t[par][:, :], t2_ps[par], ACT.Copy).then_inc(n2t_ready, 1)

            def gelu(j, par):
                act.wait_ge(f1_mm, j + 1)
                nc.scalar.activation(g_sb[par][:, :], f1_ps[par], ACT.Gelu, bias=b1_col).then_inc(gelu_ready, 1)

            normalize_1(NP - 1, 1)
            out_p(NB - 2, 0)
            out_v(NB - 2, 0)
            out_at(NB - 3, 1)
            out_n1t(NB - 1, 1)
            exps(NB - 2, 0)
            out_p(NB - 1, 1)
            out_v(NB - 1, 1)
            out_n2t(0, 0)
            out_at(NB - 2, 0)
            out_n2t(1, 1)
            exps(NB - 1, 1)
            out_at(NB - 1, 1)
            gelu(0, 0)
            with act.Fori(1, NP // 2) as m:
                for par in (1, 0):
                    out_n2t(2 * m + 1 - par, 1 - par)
                    gelu(2 * m - par, par)
            gelu(NP - 1, 1)

        @block.vector
        def _(dve):
            steps = [0]

            def chain(ins):
                steps[0] += 1
                ins.then_inc(setup_step, 1)
                dve.wait_ge(setup_step, steps[0])

            def second_tap(k, src):
                if isinstance(k, int) and k >= 1:
                    dve.wait_ge(conv_ready, k)
                dve.wait_ge(tap0_ready, k + 1)
                nc.vector.scalar_tensor_tensor(tap01[:, :], src[:, 1:T + 1], tok_w[:, D + 1:D + 2], tap0[:, :],
                                               ALU.mult, ALU.add).then_inc(tap01_ready, 1)

            def third_tap(k, src):
                dve.wait_ge(tap01_ready, k + 1)
                if after(k, 1):
                    dve.wait_ge(x_mm, 2 * k)
                nc.vector.scalar_tensor_tensor(xc[:, :], src[:, 2:T + 2], tok_w[:, D + 2:D + 3], tap01[:, :],
                                               ALU.mult, ALU.add).then_inc(conv_ready, 1)

            def scale_x(pair, par=0, m=2, src=x_ps):
                done = 2 * pair + par + m
                dve.wait_ge(rstd_x_ready, done)
                for n in range(2 * par, 2 * par + 2 * m):
                    last = nc.vector.scalar_tensor_tensor(scaled[:, n, :], src[n // 2][:, n % 2, :], rstd_x[:, n:n + 1],
                                                          gamma, ALU.mult, ALU.mult)
                last.then_inc(x_scaled, m)

            def stats_1(pair, par=0, m=2):
                dve.wait_ge(h_ready, 2 * pair + par + m)
                for n in range(2 * par, 2 * par + 2 * m):
                    last = nc.vector.bn_stats(bn1[:, n, :], h_pairs[:, pair, n * D:(n + 1) * D])
                last.then_inc(bn1_ready, m)

            def aggregate_1(par=0, m=2):
                for n in range(2 * par, 2 * par + 2 * m):
                    last = nc.vector.bn_aggr(mv1[:, n, :], bn1[:, n, :])
                last.then_inc(stats1, m)

            def head_h(pair, par, src):
                scale_x(pair, par, 1, src)
                dve.wait_ge(x_scaled, 2 * pair + par + 1)
                nc.vector.tensor_tensor(h_tiles[:, pair, 2 * par:2 * par + 2, :], scaled[:, 2 * par:2 * par + 2, :],
                                        beta_4[:, 0:2, :], ALU.add).then_inc(h_ready, 1)

            def head_stats(pair, par):
                b = 2 * pair + par
                stats_1(pair, par, 1)
                dve.wait_ge(bn1_ready, b + 1)
                if b >= 2:
                    dve.wait_ge(rstd1_ready, b - 1)
                    dve.wait_ge(n1_ready, b - 1)
                aggregate_1(par, 1)

            def head_n1(par):
                dve.wait_ge(rstd1_ready, par + 1)
                for n in (2 * par, 2 * par + 1):
                    last = nc.vector.tensor_scalar(n1[par][:, n % 2, :], h_tiles[:, 0, n, :], mv1[:, n, 0:1],
                                                   rstd1[:, n:n + 1], ALU.subtract, ALU.mult)
                last.then_inc(n1_ready, 1)

            def row_max(b, par):
                dve.wait_ge(s_mm, b + 1)
                nc.vector.tensor_reduce(neg_max[par][:, :], s_ps[par], AX_X, ALU.max, negate=True).then_inc(max_ready, 1)

            def residual(b):
                dve.wait_ge(o_mm, b + 1)
                nc.vector.reciprocal(rinv[:, :], o_ps[:, :, D]).then_inc(rinv_ready, 1)
                dve.wait_ge(rinv_ready, b + 1)
                nc.vector.tensor_tensor(rinv_keep[:, :], rinv[:, :], keep[:, :], ALU.mult).then_inc(keep_applied, 1)
                dve.wait_ge(keep_applied, b + 1)
                for a in range(2):
                    h = h_all[:, b, a * D:(a + 1) * D]
                    last = nc.vector.scalar_tensor_tensor(h, o_ps[:, a, 0:D], rinv_keep[:, a:a + 1], h,
                                                          ALU.mult, ALU.add)
                last.then_inc(resid_ready, 1)

            def stats_2(k, par):
                dve.wait_ge(resid_ready, 2 * k + 1 + par)
                for n in (2 * par, 2 * par + 1):
                    last = nc.vector.bn_stats(bn2[:, n, :], h_pairs[:, k, n * D:(n + 1) * D])
                last.then_inc(bn2_ready, 1)

            def aggregate_2():
                for n in range(4):
                    last = nc.vector.bn_aggr(mv2[:, n, :], bn2[:, n, :])
                last.then_inc(stats2, 1)

            nc.vector.memset(warm[:, :], 1.0).then_inc(warm_ready, 1)
            nc.vector.memset(mean_w[0:C, :], 1.0 / C).then_inc(mean_w_ready, 1)
            nc.vector.memset(mean_w[C:, :], 1.0).then_inc(mean_w_ready, 1)
            nc.vector.memset(ones_b[:, :], 1.0).then_inc(ones_ready, 1)
            nc.vector.memset(ones_f[:, :], 1.0).then_inc(ones_ready, 1)
            chain(nc.vector.memset(cb_rows[:, :], 0.0))
            dve.wait_ge(landed_tok, 16)
            nc.vector.tensor_reduce(lin_mean[:, :], lin_t, AX_X, ALU.add).then_inc(means_step, 1)
            nc.vector.tensor_reduce(emb_mean[:, :], emb_b, AX_X, ALU.add).then_inc(means_step, 1)
            dve.wait_ge(means_step, 2)
            nc.vector.tensor_scalar(lin_mean[:, :], lin_mean[:, :], 1.0 / D, None, ALU.mult).then_inc(means_step, 1)
            nc.vector.tensor_scalar(emb_mean[:, :], emb_mean[:, :], 1.0 / D, None, ALU.mult).then_inc(means_step, 1)
            dve.wait_ge(means_step, 4)
            nc.vector.tensor_scalar(emb_c[:, :], emb_b, emb_mean[:, :], None, ALU.subtract)\
                .then_inc(emb_centred, 1)
            second_tap(0, x_head[:, 0, :])
            nc.vector.tensor_scalar(lin_c[:, :], lin_t, lin_mean[:, :], None, ALU.subtract).then_inc(lin_centred, 1)
            third_tap(0, x_head[:, 0, :])
            dve.wait_ge(cb_mm, 1)
            cb_ps = bank_s0[0:C + 1, 0:D]
            nc.vector.tensor_copy(cb_all[:, :], bank_s0[0:H, 0:D]).then_inc(cb_all_ready, 1)
            chain(nc.vector.tensor_copy(cb_hi[:, :], cb_ps))
            chain(nc.vector.tensor_tensor(cb_rest[:, :], cb_ps, cb_hi[:, :], ALU.subtract))
            dve.wait_ge(cb_all_ready, 1)
            for par in range(2):
                dve.wait_ge(x_mm, par + 1)
                nc.vector.tensor_tensor(x_first[par][:, :, :], x_ps[par], cb_all[:, :].unsqueeze(1).broadcast_to((H, 2, D)),
                                        ALU.add).then_inc(x_first_ready, 1)
            chain(nc.vector.tensor_copy(cb_mid[:, :], cb_rest[:, :]))
            chain(nc.vector.tensor_tensor(cb_rest2[:, :], cb_rest[:, :], cb_mid[:, :], ALU.subtract))
            nc.vector.tensor_copy(cb_rows[0:1, :], cb_hi[0:1, :]).then_inc(cb_ready, 1)
            nc.vector.tensor_copy(cb_rows[32:33, :], cb_mid[32:33, :]).then_inc(cb_ready, 1)
            nc.vector.tensor_copy(cb_rows[64:65, :], cb_rest2[64:65, :]).then_inc(cb_ready, 1)
            second_tap(1, x_head[:, 1, :])
            third_tap(1, x_head[:, 1, :])
            dve.wait_ge(landed_rows, 16)
            head_h(0, 0, x_first)
            head_stats(0, 0)
            head_h(0, 1, x_first)
            head_n1(0)
            head_stats(0, 1)
            head_h(1, 0, x_ps)
            head_n1(1)
            head_stats(1, 0)
            second_tap(2, x_head[:, 2, :])
            row_max(0, 0)
            third_tap(2, x_head[:, 2, :])
            head_h(1, 1, x_ps)
            head_stats(1, 1)
            second_tap(3, x_head[:, 3, :])
            dve.wait_ge(exp_ready, 1)
            chain(nc.vector.tensor_reduce(row_sum[:, :], s_ps[0], AX_X, ALU.add))
            for a in range(2):
                last = nc.vector.tensor_scalar(sum_diag[:, a * H:(a + 1) * H], ident[0:H, 0:H], row_sum[:, a:a + 1],
                                               None, ALU.mult)
            last.then_inc(sums_diagonal, 1)
            row_max(1, 1)
            dve.wait_ge(sums_spread, 1)
            chain(nc.vector.tensor_reduce(least[:, :], sums_ps, AX_X, ALU.min))
            nc.vector.tensor_scalar(cand0[:, :], sums_ps, least[:, :], BIG, ALU.is_gt, ALU.mult).then_inc(sums_used, 1)
            third_tap(3, x_head[:, 3, :])
            scale_x(2)
            dve.wait_ge(sums_used, 1)
            dve.wait_ge(iota_ready, 2)
            chain(nc.vector.tensor_tensor(cand[:, :], cand0[:, :], token_row[:, :], ALU.add))
            chain(nc.vector.tensor_reduce(c0[:, :], cand[:, :], AX_X, ALU.min))
            nc.vector.tensor_scalar(keep[:, :], token_col[:, :], c0[:, :], None, ALU.not_equal).then_inc(keep_ready, 1)

            def from_scores(k):
                stats_2(k - 1, 0)
                residual(2 * k - 1)
                stats_2(k - 1, 1)
                scale_x(k + 2)
                dve.wait_ge(bn2_ready, 2 * k)
                row_max(2 * k + 1, 1)
                aggregate_2()

            dve.wait_ge(keep_ready, 1)
            residual(0)
            stats_1(2)
            dve.wait_ge(bn1_ready, 6)
            dve.wait_ge(shift1_ready, 2)
            aggregate_1()
            row_max(2, 0)
            second_tap(4, x_slot)
            third_tap(4, x_slot)
            from_scores(1)
            with dve.Fori(2, NP - 3) as k:
                residual(2 * k - 2)
                stats_1(k + 1)
                dve.wait_ge(bn1_ready, 2 * k + 4)
                second_tap(k + 3, x_slot)
                aggregate_1()
                third_tap(k + 3, x_slot)
                row_max(2 * k, 0)
                from_scores(k)

            def finish(j, y, first=0, m=2):
                tiles = slice(2 * first, 2 * first + 2 * m)
                dve.wait_ge(hb_ready, j + 1)
                dve.wait_ge(y_mm, 2 * j + first + m)
                nc.vector.tensor_tensor(hb_all[:, j, tiles, :], y[:, tiles, :], hb_all[:, j, tiles, :],
                                        ALU.add).then_inc(y_ready, m)

            def normalize_2(j, par):
                dve.wait_ge(mean2_ready, j + 1)
                dve.wait_ge(rstd2_ready, j + 1)
                if after(j, 2):
                    dve.wait_ge(t2_mm, j - 1)
                for n in range(4):
                    last = nc.vector.tensor_scalar(n2[par][:, n, :], h_pairs[:, j, n * D:(n + 1) * D],
                                                   mean2[:, j, n:n + 1], rstd2[:, j, n:n + 1],
                                                   ALU.subtract, ALU.mult)
                last.then_inc(n2_ready, 1)

            for k in range(NP - 3, NP):
                residual(2 * k - 2)
                if k < NP - 1:
                    stats_1(k + 1)
                    dve.wait_ge(bn1_ready, 2 * k + 4)
                    aggregate_1()
                else:
                    normalize_2(1, 1)
                row_max(2 * k, 0)
                stats_2(k - 1, 0)
                residual(2 * k - 1)
                if k < NP - 2:
                    scale_x(k + 2)
                elif k < NP - 1:
                    normalize_2(0, 0)
                row_max(2 * k + 1, 1)
                stats_2(k - 1, 1)
                dve.wait_ge(bn2_ready, 2 * k)
                dve.wait_ge(rstd2_ready, k - 1)
                aggregate_2()

            residual(NB - 2)
            stats_2(NP - 1, 0)
            normalize_2(2, 0)
            normalize_2(3, 1)
            residual(NB - 1)
            stats_2(NP - 1, 1)
            dve.wait_ge(bn2_ready, NB)
            dve.wait_ge(rstd2_ready, NP - 1)
            aggregate_2()
            for j in range(4, NP):
                normalize_2(j, j % 2)
                finish(j - 4, y_ps[j % 2])
            for j in range(NP - 4, NP - 1):
                finish(j, y_ps[j % 2])
            finish(NP - 1, y_ps[1], 0, 1)
            finish(NP - 1, y_last_ps, 1, 1)


def kernel(x, L0_tok_conv_w, L0_tok_conv_b, L0_tok_lin_w, L0_tok_lin_b, L0_tok_emb, L0_tok_ln_g, L0_tok_ln_b,
           L0_attn_kernel, L0_ffn_W1, L0_ffn_b1, L0_ffn_W2, L0_ffn_b2):
    import numpy as np
    import concourse.bacc as bacc
    from concourse.bass_utils import run_bass_kernel_spmd

    tok = np.concatenate([L0_tok_lin_w.T, L0_tok_conv_w[:, 0, :], L0_tok_conv_b[:, None]], axis=1)
    emb = np.concatenate([L0_tok_emb, L0_tok_lin_b[None, :],
                          np.zeros((2 * tok.shape[0] - L0_tok_emb.shape[0] - 1, L0_tok_emb.shape[1]), L0_tok_emb.dtype)])
    arrays = {
        "x_dram": np.ascontiguousarray(x),
        "tok_dram": np.ascontiguousarray(np.concatenate([np.concatenate([tok, tok], axis=0), emb], axis=1)),
        "weights_dram": np.ascontiguousarray(np.concatenate(
            [L0_attn_kernel[0].T, L0_attn_kernel[1].T, L0_attn_kernel[2], L0_ffn_W1.T, L0_ffn_W2.T,
             L0_ffn_b1[:, None]], axis=1)),
        "rows_dram": np.ascontiguousarray(np.concatenate([L0_tok_ln_g, L0_tok_ln_b, L0_ffn_b2])[None, :]),
    }
    nc = bacc.Bacc("TRN2", target_bir_lowering=False, num_devices=1)
    args = [nc.dram_tensor(n, a.shape, mybir.dt.from_np(a.dtype), kind="ExternalInput").ap()
            for n, a in arrays.items()]
    out_shape = (x.shape[0], x.shape[2], L0_tok_lin_w.shape[0])
    args.append(nc.dram_tensor("out_dram", out_shape, F32, kind="ExternalOutput").ap())
    audio_tower(nc, *args)
    r = run_bass_kernel_spmd(nc, [arrays], core_ids=[0])
    return r.results[0]["out_dram"]
```
